# Optimizing a Trainium2 kernel written in Bass

```python
import numpy as np
import jax
import jax.numpy as jnp

def _softmax(x, axis=-1):
    return jax.nn.softmax(x, axis=axis)

def _gelu(x):
    return jax.nn.gelu(x, approximate=True)

def _silu(x):
    return jax.nn.silu(x)

def _sigmoid(x):
    return jax.nn.sigmoid(x)

def _layernorm(x, axis=-1, eps=1e-05):
    m = jnp.mean(x, axis=axis, keepdims=True)
    v = jnp.var(x, axis=axis, keepdims=True)
    return (x - m) / jnp.sqrt(v + eps)

def _scatter_add(tgt, idx, src, axis=0):
    return tgt.at[idx].add(src)

def _segment_sum(src, seg, n):
    return jax.ops.segment_sum(src, seg, n)
kernel_name = 'mk_adj_seq_d2_adj_r2_e0c559'

def setup_inputs(seed: int=0):
    np.random.seed(seed)
    _w = jnp.asarray

    def _rec_inputs():
        import jax
        import jax.numpy as jnp
        _gk = jax.random.key(seed)
        x = -0.0005207 + 1.001 * jax.random.normal(jax.random.fold_in(_gk, 1), (8, 1024, 128), jnp.float32)
        _w = (1.0 + jnp.arange(1024, dtype=jnp.float32)) ** (-0.5)
        _w = _w / _w.mean()
        _pij = jnp.clip(0.00195312 * _w[:, None] * _w[None, :], 0.0, 1.0)
        _a = jax.random.uniform(jax.random.fold_in(_gk, 2), (8, 1024, 1024)) < _pij
        adj = _a.astype(jnp.int32)
        return (x, adj)
    x, adj = _rec_inputs()

    def _L0_gnn_setup():
        import jax, jax.numpy as jnp
        import numpy as np
        ALPHA = 0.2
        NEG = -9000000000000000.0
        EPS = 1e-05

        def _gat(h, adj, W, a, out_features):
            Wh = jnp.matmul(h, W)
            Wh1 = jnp.matmul(Wh, a[:out_features])
            Wh2 = jnp.matmul(Wh, a[out_features:])
            e = Wh1 + jnp.swapaxes(Wh2, 1, 2)
            e = jax.nn.leaky_relu(e, negative_slope=ALPHA)
            scores = jnp.where(adj > 0, e, NEG)
            att = jax.nn.softmax(scores, axis=1)
            return jnp.matmul(att, Wh)

        def _layernorm(x, g, b):
            mu = jnp.mean(x, axis=-1, keepdims=True)
            var = jnp.var(x, axis=-1, keepdims=True)
            return (x - mu) * jax.lax.rsqrt(var + EPS) * g + b
        key = jax.random.key(seed)
        ks = jax.random.split(key, 8)
        B, N, F, H = (2, 2048, 128, 512)
        x = jax.random.normal(ks[0], (B, N, F), dtype=jnp.float32)
        adj = jax.random.randint(ks[1], (B, N, N), 0, 2, dtype=jnp.int32)

        def xavier(k, shape):
            fan_in, fan_out = (shape[0], shape[1])
            lim = np.sqrt(6.0 / (fan_in + fan_out))
            return jax.random.uniform(k, shape, jnp.float32, -lim, lim)
        return {'x': x, 'adj': adj, 'W1': xavier(ks[2], (F, F)), 'a1': xavier(ks[3], (2 * F, 1)), 'W2': xavier(ks[4], (F, F)), 'a2': xavier(ks[5], (2 * F, 1)), 'w_ff1': xavier(ks[6], (F, H)), 'b_ff1': jnp.zeros((H,), jnp.float32), 'w_ff2': xavier(ks[7], (H, F)), 'b_ff2': jnp.zeros((F,), jnp.float32), 'g_ln1': jnp.ones((F,), jnp.float32), 'b_ln1': jnp.zeros((F,), jnp.float32), 'g_ln2': jnp.ones((F,), jnp.float32), 'b_ln2': jnp.zeros((F,), jnp.float32)}
    _L0_gnn_all = _L0_gnn_setup()
    _L0_gnn_in = {k: v for k, v in _L0_gnn_all.items() if k in ('W1', 'a1', 'W2', 'a2', 'w_ff1', 'b_ff1', 'w_ff2', 'b_ff2', 'g_ln1', 'b_ln1', 'g_ln2', 'b_ln2')}
    del _L0_gnn_all

    def _L1_gnn_setup():
        import jax, jax.numpy as jnp
        import numpy as np
        B, N, D = (8, 512, 128)
        H = 8
        DH = D // H
        R = 4
        FF = 512
        EPS = 1e-05

        def _lin(k, fan_in, shape):
            return jax.random.normal(k, shape, jnp.float32) * (1.0 / np.sqrt(fan_in))

        def _ln(x, g, b):
            m = x.mean(-1, keepdims=True)
            v = ((x - m) ** 2).mean(-1, keepdims=True)
            return (x - m) * jax.lax.rsqrt(v + EPS) * g + b
        key = jax.random.key(seed)
        ks = jax.random.split(key, 16)
        src = jax.random.normal(ks[0], (B, N, D), jnp.float32)
        adj_matrix = jax.random.randint(ks[1], (B, N, N), 0, 5, dtype=jnp.int32)
        Wq = _lin(ks[2], D, (D, D))
        bq = jnp.zeros((D,), jnp.float32)
        Wk = _lin(ks[3], D, (D, D))
        bk = jnp.zeros((D,), jnp.float32)
        Wv = _lin(ks[4], D, (R, D, D))
        bv = jnp.zeros((R, D), jnp.float32)
        Wo = _lin(ks[5], D, (D, D))
        bo = jnp.zeros((D,), jnp.float32)
        W1 = _lin(ks[6], D, (D, FF))
        b1 = jnp.zeros((FF,), jnp.float32)
        W2 = _lin(ks[7], FF, (FF, D))
        b2 = jnp.zeros((D,), jnp.float32)
        g1 = jnp.ones((D,), jnp.float32)
        beta1 = jnp.zeros((D,), jnp.float32)
        g2 = jnp.ones((D,), jnp.float32)
        beta2 = jnp.zeros((D,), jnp.float32)
        return dict(src=src, adj_matrix=adj_matrix, Wq=Wq, bq=bq, Wk=Wk, bk=bk, Wv=Wv, bv=bv, Wo=Wo, bo=bo, W1=W1, b1=b1, W2=W2, b2=b2, g1=g1, beta1=beta1, g2=g2, beta2=beta2)
    _L1_gnn_all = _L1_gnn_setup()
    _L1_gnn_in = {k: v for k, v in _L1_gnn_all.items() if k in ('Wq', 'bq', 'Wk', 'bk', 'Wv', 'bv', 'Wo', 'bo', 'W1', 'b1', 'W2', 'b2', 'g1', 'beta1', 'g2', 'beta2')}
    del _L1_gnn_all
    return {'x': x, 'adj': adj, 'L0_gnn_W1': _L0_gnn_in['W1'], 'L0_gnn_a1': _L0_gnn_in['a1'], 'L0_gnn_W2': _L0_gnn_in['W2'], 'L0_gnn_a2': _L0_gnn_in['a2'], 'L0_gnn_w_ff1': _L0_gnn_in['w_ff1'], 'L0_gnn_b_ff1': _L0_gnn_in['b_ff1'], 'L0_gnn_w_ff2': _L0_gnn_in['w_ff2'], 'L0_gnn_b_ff2': _L0_gnn_in['b_ff2'], 'L0_gnn_g_ln1': _L0_gnn_in['g_ln1'], 'L0_gnn_b_ln1': _L0_gnn_in['b_ln1'], 'L0_gnn_g_ln2': _L0_gnn_in['g_ln2'], 'L0_gnn_b_ln2': _L0_gnn_in['b_ln2'], 'L1_gnn_Wq': _L1_gnn_in['Wq'], 'L1_gnn_bq': _L1_gnn_in['bq'], 'L1_gnn_Wk': _L1_gnn_in['Wk'], 'L1_gnn_bk': _L1_gnn_in['bk'], 'L1_gnn_Wv': _L1_gnn_in['Wv'], 'L1_gnn_bv': _L1_gnn_in['bv'], 'L1_gnn_Wo': _L1_gnn_in['Wo'], 'L1_gnn_bo': _L1_gnn_in['bo'], 'L1_gnn_W1': _L1_gnn_in['W1'], 'L1_gnn_b1': _L1_gnn_in['b1'], 'L1_gnn_W2': _L1_gnn_in['W2'], 'L1_gnn_b2': _L1_gnn_in['b2'], 'L1_gnn_g1': _L1_gnn_in['g1'], 'L1_gnn_beta1': _L1_gnn_in['beta1'], 'L1_gnn_g2': _L1_gnn_in['g2'], 'L1_gnn_beta2': _L1_gnn_in['beta2']}

def reference(x, adj, L0_gnn_W1, L0_gnn_a1, L0_gnn_W2, L0_gnn_a2, L0_gnn_w_ff1, L0_gnn_b_ff1, L0_gnn_w_ff2, L0_gnn_b_ff2, L0_gnn_g_ln1, L0_gnn_b_ln1, L0_gnn_g_ln2, L0_gnn_b_ln2, L1_gnn_Wq, L1_gnn_bq, L1_gnn_Wk, L1_gnn_bk, L1_gnn_Wv, L1_gnn_bv, L1_gnn_Wo, L1_gnn_bo, L1_gnn_W1, L1_gnn_b1, L1_gnn_W2, L1_gnn_b2, L1_gnn_g1, L1_gnn_beta1, L1_gnn_g2, L1_gnn_beta2):
    import jax
    import jax.numpy as jnp

    def _L0_gnn_ref(x, adj, W1, a1, W2, a2, w_ff1, b_ff1, w_ff2, b_ff2, g_ln1, b_ln1, g_ln2, b_ln2):
        import jax, jax.numpy as jnp
        import numpy as np
        ALPHA = 0.2
        NEG = -9000000000000000.0
        EPS = 1e-05

        def _gat(h, adj, W, a, out_features):
            Wh = jnp.matmul(h, W)
            Wh1 = jnp.matmul(Wh, a[:out_features])
            Wh2 = jnp.matmul(Wh, a[out_features:])
            e = Wh1 + jnp.swapaxes(Wh2, 1, 2)
            e = jax.nn.leaky_relu(e, negative_slope=ALPHA)
            scores = jnp.where(adj > 0, e, NEG)
            att = jax.nn.softmax(scores, axis=1)
            return jnp.matmul(att, Wh)

        def _layernorm(x, g, b):
            mu = jnp.mean(x, axis=-1, keepdims=True)
            var = jnp.var(x, axis=-1, keepdims=True)
            return (x - mu) * jax.lax.rsqrt(var + EPS) * g + b
        Fout = W1.shape[1]
        residual = x
        h = _gat(x, adj, W1, a1, Fout)
        h = _gat(h, adj, W2, a2, W2.shape[1])
        h = _layernorm(residual + h, g_ln1, b_ln1)
        residual2 = h
        ff = jnp.matmul(jax.nn.relu(jnp.matmul(h, w_ff1) + b_ff1), w_ff2) + b_ff2
        return _layernorm(residual2 + ff, g_ln2, b_ln2)

    def _L1_gnn_ref(src, adj_matrix, Wq, bq, Wk, bk, Wv, bv, Wo, bo, W1, b1, W2, b2, g1, beta1, g2, beta2):
        import jax, jax.numpy as jnp
        import numpy as np
        B, N, D = (8, 512, 128)
        H = 8
        DH = D // H
        R = 4
        FF = 512
        EPS = 1e-05

        def _lin(k, fan_in, shape):
            return jax.random.normal(k, shape, jnp.float32) * (1.0 / np.sqrt(fan_in))

        def _ln(x, g, b):
            m = x.mean(-1, keepdims=True)
            v = ((x - m) ** 2).mean(-1, keepdims=True)
            return (x - m) * jax.lax.rsqrt(v + EPS) * g + b
        Bb, Nn, Dm = src.shape
        h, dh = (H, Dm // H)
        q = (src @ Wq + bq).reshape(Bb, Nn, h, dh).transpose(0, 2, 1, 3)
        k = (src @ Wk + bk).reshape(Bb, Nn, h, dh).transpose(0, 2, 1, 3)
        scores = jnp.einsum('bhid,bhjd->bhij', q, k) / np.sqrt(dh)
        attn = jax.nn.softmax(scores, axis=-1)
        out = jnp.zeros_like(q)
        for r in range(Wv.shape[0]):
            v_r = (src @ Wv[r] + bv[r]).reshape(Bb, Nn, h, dh).transpose(0, 2, 1, 3)
            mask = (adj_matrix == r)[:, None]
            out = out + jnp.einsum('bhij,bhjd->bhid', attn * mask, v_r)
        attn_out = out.transpose(0, 2, 1, 3).reshape(Bb, Nn, Dm) @ Wo + bo
        x = _ln(src + attn_out, g1, beta1)
        ff = jax.nn.gelu(x @ W1 + b1, approximate=False) @ W2 + b2
        return _ln(x + ff, g2, beta2)
    x = _L0_gnn_ref(x, adj, L0_gnn_W1, L0_gnn_a1, L0_gnn_W2, L0_gnn_a2, L0_gnn_w_ff1, L0_gnn_b_ff1, L0_gnn_w_ff2, L0_gnn_b_ff2, L0_gnn_g_ln1, L0_gnn_b_ln1, L0_gnn_g_ln2, L0_gnn_b_ln2)
    x = _L1_gnn_ref(x, adj, L1_gnn_Wq, L1_gnn_bq, L1_gnn_Wk, L1_gnn_bk, L1_gnn_Wv, L1_gnn_bv, L1_gnn_Wo, L1_gnn_bo, L1_gnn_W1, L1_gnn_b1, L1_gnn_W2, L1_gnn_b2, L1_gnn_g1, L1_gnn_beta1, L1_gnn_g2, L1_gnn_beta2)
    return x

_drawn_inputs = setup_inputs


def setup_inputs(seed=0):
    import zlib

    import numpy as np

    out = dict(_drawn_inputs(seed))
    spreads = {'L0_gnn_b_ff1': (0.0, 0.1),
     'L0_gnn_b_ff2': (0.0, 0.1),
     'L0_gnn_g_ln1': (1.0, 0.2),
     'L0_gnn_b_ln1': (0.0, 0.1),
     'L0_gnn_g_ln2': (1.0, 0.2),
     'L0_gnn_b_ln2': (0.0, 0.1),
     'L1_gnn_bq': (0.0, 0.8),
     'L1_gnn_bk': (0.0, 0.8),
     'L1_gnn_bv': (0.0, 0.1),
     'L1_gnn_bo': (0.0, 0.1),
     'L1_gnn_b1': (0.0, 0.1),
     'L1_gnn_b2': (0.0, 0.1),
     'L1_gnn_g1': (1.0, 0.2),
     'L1_gnn_beta1': (0.0, 0.1),
     'L1_gnn_g2': (1.0, 0.2),
     'L1_gnn_beta2': (0.0, 0.1)}
    factors = {}
    for name, (base, spread) in spreads.items():
        noise = np.random.default_rng([zlib.crc32(name.encode()), seed]).standard_normal(out[name].shape)
        drawn = base * np.exp(spread * noise) if base else spread * noise
        out[name] = jnp.asarray(drawn.astype(out[name].dtype))
    for name, factor in factors.items():
        out[name] = (out[name] * factor).astype(out[name].dtype)
    return out
```

```python
import concourse.bass as bass
from concourse import mybir
from contextlib import ExitStack

F32 = mybir.dt.float32
BF16 = mybir.dt.bfloat16
I32 = mybir.dt.int32
U8 = mybir.dt.uint8
ALU = mybir.AluOpType
ACT = mybir.ActivationFunctionType
AX = mybir.AxisListType

P = 128
B, N, F = 8, 1024, 128
HID = 512
NH, DH = 8, 16
VW = DH + 1
NT = N // P
HALF = 512
NHALF = N // HALF
HC = HID // P
EPS = 1e-5
FAR = 2.0 ** 100
QK_PIECES = [(0, 0), (0, 1), (1, 0), (1, 1), (0, 2), (2, 0)]
KROWS = 16 * len(QK_PIECES)
CROWS = 3
SROWS = KROWS + CROWS
STEPS = NT * NHALF * 2
MAX_CHUNKS = 2

COLS = {}
for _name, _n in (("bff1", HC), ("bff2", 1), ("gln1", 1), ("bln1", 1), ("gln2", 1), ("bln2", 1),
                  ("bq", 1), ("bk", 1), ("bo", 1), ("b1", HC), ("b2", 1),
                  ("g1", 1), ("be1", 1), ("g2", 1), ("be2", 1),
                  ("a1s", 1), ("a1t", 1), ("a2s", 1), ("a2t", 1)):
    COLS[_name] = (sum(n for _, n in COLS.values()), _n)
NCOLS = sum(n for _, n in COLS.values())


def bank_plan():
    def ln(i):
        return [("xc", i, 0), ("xc", i, 1), ("var", i), ("bc", i, 0), ("bc", i, 1)]

    def ff(i):
        out = []
        for half in range(2):
            out += [("f1", i, half, 0), ("f1", i, half, 1), ("f2", i, half)]
            out += [("f1", i, half, c) for c in range(2, HC)]
        return out

    pre = []
    for k in range(2):
        pre += [("s", k, i) for i in range(2)] + [("wh", k, i) for i in range(3)]
        pre += [("gout", k, i) for i in range(2)]
    pre += [("fl",)] + ln(0) + ff(0) + ln(1) + [(w, half) for w in "qk" for half in range(2)]
    post = [("sm",)] + [("rb", gi) for gi in range(4)] + [("wo", half) for half in range(2)] + ln(2) + ff(1) + ln(3)
    values = [("v", i) for i in range(NT // 2)]
    plan, used = {}, {}
    for part, keys in (("pre", pre), ("val", values), ("post", post)):
        used[part] = [0, 0, 0]
        for n, key in enumerate(keys):
            bank = n % 3
            plan[key] = (part, bank, used[part][bank])
            used[part][bank] += 1
    return plan, used


def build(nc, xT, adjT, mats, wv, wo, cols, bv, outT):
    nc.disable_value_cache = True
    ctx = ExitStack()
    with ctx:
        def sb(name, shape, dt=F32):
            return ctx.enter_context(nc.sbuf_tensor(name, shape, dt))

        def ps(name, shape, dt=F32):
            return ctx.enter_context(nc.psum_tensor(name, shape, dt))

        MAT = sb("MAT", [P, mats.shape[1]])
        off = [0]

        def mat(width):
            off[0] += width
            return MAT[:, off[0] - width:off[0]]

        gW = [mat(P), mat(P)]
        gWT = [mat(P), mat(P)]
        wff1 = mat(HID)
        wff2 = mat(HID).rearrange("p (c f) -> p c f", c=HC)
        Wq = mat(P)
        Wk = mat(P)
        W1 = mat(HID)
        W2 = mat(HID).rearrange("p (c f) -> p c f", c=HC)
        WV = sb("WV", [P, 2, P])
        WO = sb("WO", [P, 2, P])
        COL = sb("COL", [P, NCOLS])
        BQ4 = sb("BQ4", [P, 1])
        BVD = sb("BVD", [P, 2, P])
        WREP = sb("WREP", [P, 2, P])
        WX = sb("WX", [P, 2, P + 1])
        CEN = sb("CEN", [P, P])
        MEAN = sb("MEAN", [P, P])
        SEL = sb("SEL", [P, 4])
        IDF = sb("IDF", [P, P])
        POW = sb("POW", [P, NT])
        IDB = sb("IDB", [P, P], BF16)
        HALFN = sb("HALFN", [P, 1])
        WVX = sb("WVX", [P, 3, P])
        BVX = sb("BVX", [P, 3, P])

        def col(name, c=0):
            return COL[:, COLS[name][0] + c:COLS[name][0] + c + 1]

        QS = sb("QS", [P, NH, N], BF16)
        KS = sb("KS", [P, NH, N], BF16)
        VV = sb("VV", [P, NT * 2 * NH * VW + 32])
        V4 = VV[:, 0:NT * 2 * NH * VW].rearrange("p (t w h d) -> p t w h d", t=NT, w=2, h=NH)
        M1 = sb("M1", [P, NT, N], U8)
        MX = sb("MX", [P, 2, NT, 4])
        MNEG = sb("MNEG", [P, 2, NT, 4])
        MR = sb("MR", [P, 2, NT, 4])
        CM = sb("CM", [P, 2, NT, CROWS, 4], BF16)
        CR = sb("CR", [CROWS * 4, N], BF16)
        PT = sb("PT", [P, 3, 4, HALF])
        PM = sb("PM", [P, 2, 4, HALF])
        U = sb("U", [P, 4, HALF])
        RES = sb("RES", [P, N])
        FLAG = sb("FLAG", [P, 1], I32)
        VC = sb("VC", [P, 3, 4, 32])
        XB = PT[:, 2, 1, 0:P]
        AR = PT[:, 2, 0, :].bitcast(I32)
        MK, BELOW = PT[:, 1, 0:3, :], PT[:, 1, 3, :]
        WVR = PT[:, 0, 0, :].rearrange("p (r f) -> p r f", r=4)
        BV = PT[:, 0, 1, :].rearrange("p (r f) -> p r f", r=4)
        AREP = PT[:, 0, 2, 0:2 * P].rearrange("p (k f) -> p k f", k=2)
        ZERO = PT[:, 0, 3, 0:P]

        XT = sb("XT", [P, N])
        AC = sb("AC", [P, MAX_CHUNKS, N], I32)
        NM = sb("NM", [P, NT, N], BF16)
        M1S = sb("M1S", [P, NT, N], U8)
        WH = sb("WH", [P, NT, P + 1])
        WHS = sb("WHS", [P, 4, P])
        LMIN = sb("LMIN", [P, NT])
        ESUM = sb("ESUM", [P, NT])
        ERCP = sb("ERCP", [P, NT])
        H1 = sb("H1", [P, N])
        X2 = H1
        VE = sb("VE", [P, NT])
        RS = sb("RS", [P, NT])
        RCP = sb("RCP", [P, 16, 4])
        SEEN = sb("SEEN", [P, N], BF16)
        CHK = sb("CHK", [P, NT])
        FMAX = sb("FMAX", [P, 1])
        REG = sb("REG", [P, 16, HALF])

        def rows(first, n):
            return REG[:, first:first + n, :].rearrange("p a n -> p (a n)")

        E = [REG[:, 2 * i:2 * i + 2, :] for i in range(3)]
        LP = [rows(6 + 2 * i, 2) for i in range(3)]
        SN = rows(12, 2)
        SN2 = rows(14, 2)
        FA = REG[:, 0:4, :]
        SQ, XC = FA[:, 0:2, :], FA[:, 2:4, :]
        QK = FA.rearrange("p (w a) n -> p w (a n)", w=2)
        YT = rows(6, 2)
        OT = YT
        HT = rows(8, 2)
        QP = REG[:, 10:16, :].rearrange("p a n -> p (a n)").bitcast(BF16).rearrange(
            "p (w c n) -> p w c n", w=2, c=3)

        ms = [ps(f"ms{i}", [P, HALF]) for i in range(3)]
        pv = ps("pv", [P, HALF])
        st = [ps(f"st{i}", [P, 2, HALF]) for i in range(2)]
        plan, used = bank_plan()

        adj_t = adjT.rearrange("b (t p) (i n) -> b t p i n", p=P, n=HALF)

        per = {}
        sems = {}

        def sem(name, n=1):
            sems[name] = ctx.enter_context(nc.semaphore(name))
            per[name] = n
            return name

        for part in ("pre", "val", "post"):
            for i in range(3):
                sem(f"{part}_full{i}", used[part][i])
                sem(f"{part}_free{i}", used[part][i])
        for i in range(MAX_CHUNKS):
            sem(f"chunk_in{i}", 16 * len(range(i, NT, MAX_CHUNKS)))
        for name, n in (
            ("x_in", 16), ("chunk_used", NT), ("chunk_seen", NT), ("m1_in", 16), ("res_ready", 1),
            ("sn_ready", 4), ("lp_ready", 2 * NT), ("lm_ready", 2 * NT), ("e_ready", 2 * NT),
            ("rcp_ready", 2 * NT), ("whs_ready", 2 * NT), ("e_used", 2 * (NT - 1)),
            ("pre_rs", 2), ("post_rs", 2), ("pre_ln", 4), ("post_ln", 4), ("rx_ready", 4),
            ("p1_ready", 2), ("r1_ready", 2), ("p2_ready", 2), ("p3_ready", 2),
            ("stack_in0", 16 * 2 * len(QK_PIECES)), ("stack_in1", 16 * 2 * len(QK_PIECES)),
            ("mx_full", 8 * NT), ("mx_read", 8 * NT),
            ("mneg_ready", 2), ("c1_ready", 2), ("mr_ready", 2), ("c2_ready", 2), ("cm_ready", 2),
            ("ct_full", 2), ("ct_read", 2), ("c_in", 2 * 16 * CROWS),
            ("st_full", 64), ("p_ready", 64), ("pm_ready", 64), ("p_used", 32), ("u_ready", 4),
            ("out_done", 16), ("flag_ready", 1), ("u_done", 2),
            ("r_adj", 16 * STEPS), ("r_xb", STEPS), ("r_v", STEPS), ("r_vc", STEPS), ("r_st", STEPS), ("r_p", STEPS),
            ("r_below", STEPS), ("r_mask", STEPS), ("r_pm", 3 * STEPS), ("r_acc", 3 * STEPS), ("r_done", STEPS),
        ):
            sem(name, n)
        w_in = ctx.enter_context(nc.semaphore("w_in"))
        made = ctx.enter_context(nc.semaphore("made"))
        dmade = ctx.enter_context(nc.semaphore("dmade"))
        flag_seen = ctx.enter_context(nc.semaphore("flag_seen"))
        chunk_there = ctx.enter_context(nc.semaphore("chunk_there"))
        lp_seen = ctx.enter_context(nc.semaphore("lp_seen"))
        wo_zero = ctx.enter_context(nc.semaphore("wo_zero"))
        pmade = ctx.enter_context(nc.semaphore("pmade"))
        prep_full = ctx.enter_context(nc.semaphore("prep_full"))

        AHEAD = {"r_done"}

        def graph_of(g, shift):
            return g[0], g[1] + shift

        def is_first(g):
            return isinstance(g[0], int) and g[0] + g[1] == 0

        def at(name, b, n):
            return sems[name], b[0] * per[name] + (b[1] * per[name] + n + (name in AHEAD))

        def bank_idle(b, key):
            part, i, n = plan[key]
            return at(f"{part}_free{i}", b, n)

        def first_use(key):
            return plan[key][2] == 0

        def bank_full(b, key):
            part, i, n = plan[key]
            return at(f"{part}_full{i}", b, n + 1)

        def bank_read(b, key):
            part, i, n = plan[key]
            return at(f"{part}_free{i}", b, n + 1)

        def full(key):
            return sems[f"{plan[key][0]}_full{plan[key][1]}"]

        def free(key):
            return sems[f"{plan[key][0]}_free{plan[key][1]}"]

        def bank(key):
            return ms[plan[key][1]]

        def hs(half):
            return slice(half * HALF, (half + 1) * HALF)

        def at_step(name, step, n):
            return sems[name], step * (per[name] // STEPS) + n + (name in AHEAD)

        def v_of(t, w, h):
            first = ((t * 2 + w) * NH + h) * VW
            return VV[:, first:first + 32]

        def step_number(b, g, t, it):
            return (((b[0] + b[1]) * 2 + g) * NT + t) * NHALF + it

        MAX_TICKS = NH * NT
        MAX_EXTRA = 8
        ATT_EXTRA = 3
        ATT = 4 * NT

        def side_steps(tick):
            if tick < MAX_TICKS:
                return 1 + (tick % MAX_EXTRA == MAX_EXTRA - 1)
            return 1 + (tick % ATT_EXTRA == ATT_EXTRA - 1)

        def turn(side, tick):
            for _ in range(side_steps(tick)):
                next(side, None)

        NW = 4 + NH
        block = ctx.enter_context(nc.Block())

        VAL, HEAD, LN, FF, GAT, QKV, SPLIT = NT // 2 + 1, 11, 9, 18, 9 + NT, 4, 8

        def idle(steps):
            for _ in range(steps):
                yield

        MASK_STEPS = [0, 6, 12] + [VAL + HEAD + LN + i for i in (-3, 3, 9, 15)] + [VAL + HEAD + LN + FF + LN - 4]

        def val_and_post(parts, b, has_post):
            val, post = parts[:2]
            yield from val(b, has_post)
            if has_post:
                yield from post(graph_of(b, -1), True)

        def side_of(parts, b, has_post, has_pre):
            val, post, pre = parts[:3]
            early = val_and_post(parts, b, has_post)
            if has_post and has_pre and len(parts) > 3:
                for step in range(VAL + HEAD + 2 * LN + FF):
                    if step in MASK_STEPS:
                        parts[3](graph_of(b, 1), MASK_STEPS.index(step))
                    next(early, None)
                    yield
            yield from early
            if has_pre:
                yield from pre(graph_of(b, 1), has_post)

        @block.sync
        def _(sp):
            sp.dma_start(MAT[:, :], mats).then_inc(w_in, 16)
            sp.dma_start(COL[:, :], cols).then_inc(w_in, 16)
            sp.dma_start(WVR, wv).then_inc(w_in, 16)
            sp.dma_start(BV, bv.rearrange("(o r) f -> o r f", o=1).to_broadcast([P, 4, P])).then_inc(w_in, 16)
            sp.wait_ge(wo_zero, 1)
            for h in range(NH):
                sp.dma_start(WO[32 * (h % 4):32 * (h % 4) + DH, h // 4, :], wo[h * DH:(h + 1) * DH, :]).then_inc(w_in, 16)

            def load_x(b, first):
                if not first:
                    sp.wait_ge(*bank_read(graph_of(b, -1), ("gout", 1, 1)))
                sp.dma_start(XT[:, :], xT[b[0] + b[1]]).then_inc(sems["x_in"], 16)

            def load_chunk(b, t, first):
                if t >= MAX_CHUNKS:
                    sp.wait_ge(*at("chunk_used", b, t - MAX_CHUNKS + 1))
                    sp.wait_ge(*at("chunk_seen", b, t - MAX_CHUNKS + 1))
                elif not first:
                    sp.wait_ge(*at("chunk_used", b, 0))
                    sp.wait_ge(*at("chunk_seen", b, 0))
                sp.dma_start(AC[:, t % MAX_CHUNKS, :], adjT[b[0] + b[1], t * P:(t + 1) * P, :]).then_inc(
                    sems[f"chunk_in{t % MAX_CHUNKS}"], 16)

            def stack(b, g):
                for piece, ready in ((0, "p1_ready"), (1, "p2_ready"), (2, "p3_ready")):
                    for w, dst in enumerate((QS, KS)):
                        sp.wait_ge(*at(ready, b, w + 1))
                        for slot, pair in enumerate(QK_PIECES):
                            if pair[w] == piece:
                                sp.dma_start(dst[slot * DH:(slot + 1) * DH, 4 * g:4 * g + 4, :],
                                             QP[64 * g:64 * g + 64, w, piece, :]).then_inc(sems[f"stack_in{g}"], 16)

            def negated_maxima(b, g):
                sp.wait_ge(*at("ct_read", b, g + 1))
                for c in range(CROWS):
                    sp.dma_start(QS[KROWS + c:KROWS + c + 1, 4 * g:4 * g + 4, :],
                                 CR[4 * c:4 * c + 4, :]).then_inc(sems["c_in"], 16)

            def prefetch(b, first):
                load_x(b, first)
                for t in range(MAX_CHUNKS):
                    load_chunk(b, t, first)

            def val(b, has_post):
                yield from idle(VAL)

            def post(b, in_loop):
                yield from idle(HEAD + 2 * LN + FF)
                sp.wait_ge(*at("post_ln", b, 4))
                sp.dma_start(outT[b[0] + b[1]], OT[:, :]).then_inc(sems["out_done"], 16)

            def early_load(b, t):
                if t >= 1 and t - 1 + MAX_CHUNKS < NT:
                    load_chunk(b, t - 1 + MAX_CHUNKS, False)

            def pre(b, has_post):
                yield from idle(5)
                for t in range(GAT - 5):
                    if not has_post and t + MAX_CHUNKS < NT:
                        load_chunk(b, t + MAX_CHUNKS, False)
                    yield
                yield from idle(GAT + 2 * LN + FF + QKV + SPLIT)

            def main(b, has_post, has_pre):
                side = side_of((val, post, pre, early_load), b, has_post, has_pre)
                if has_post:
                    sp.wait_ge(*at("u_done", b, 0))
                sp.wait_ge(*at("chunk_used", b, NT))
                sp.dma_start(M1[:, :, :], M1S[:, :, :]).then_inc(sems["m1_in"], 16)
                stack(b, 1)
                if has_pre:
                    prefetch(graph_of(b, 1), False)
                for tick in range(MAX_TICKS):
                    if tick == MAX_TICKS // 2 + 4:
                        negated_maxima(b, 0)
                    turn(side, tick)
                for n in range(ATT):
                    if n == 1:
                        negated_maxima(b, 1)
                    next(side, None)
                    turn(side, MAX_TICKS + n)
                for _ in side:
                    pass
                if has_pre:
                    sp.wait_ge(*at("u_done", b, 1))
                    stack(graph_of(b, 1), 0)

            prefetch((0, 0), True)
            for _ in pre((0, 0), False):
                pass
            stack((0, 0), 0)
            main((0, 0), False, True)
            with sp.Fori(0, B - 2) as c:
                main((c, 1), True, True)
            main((0, B - 1), True, False)
            for _ in post((0, B - 1), False):
                pass
            sp.wait_ge(*at("out_done", (0, B), 0))

        @block.gpsimd
        def _(pool):
            nc.gpsimd.memset(ZERO, 0.0).then_inc(pmade, 1)
            nc.gpsimd.memset(POW[:, :], -0.5).then_inc(pmade, 1)
            nc.gpsimd.memset(IDF[:, :], 0.0).then_inc(pmade, 1)
            nc.gpsimd.memset(MEAN[:, :], 1.0 / F).then_inc(pmade, 1)
            nc.gpsimd.memset(CEN[:, :], -1.0 / F).then_inc(pmade, 1)
            nc.gpsimd.memset(IDB[:, :], 0.0).then_inc(pmade, 1)
            nc.gpsimd.memset(SEL[:, :], 0.0).then_inc(pmade, 1)
            pool.wait_ge(pmade, 7)
            nc.gpsimd.affine_select(out=CEN[:, :], in_=CEN[:, :], compare_op=ALU.not_equal, fill=1.0 - 1.0 / F,
                                    base=0, pattern=[[-1, P]], channel_multiplier=1).then_inc(pmade, 1)
            nc.gpsimd.affine_select(out=IDB[:, :], in_=IDB[:, :], compare_op=ALU.not_equal, fill=1.0,
                                    base=0, pattern=[[-1, P]], channel_multiplier=1).then_inc(pmade, 1)
            nc.gpsimd.affine_select(out=IDF[:, :], in_=IDF[:, :], compare_op=ALU.not_equal, fill=1.0,
                                    base=0, pattern=[[-1, P]], channel_multiplier=1).then_inc(pmade, 1)
            nc.gpsimd.affine_select(out=SEL[:, :], in_=SEL[:, :], compare_op=ALU.not_equal, fill=1.0, base=-DH,
                                    pattern=[[-32, 4]], channel_multiplier=1).then_inc(pmade, 1)

            def ln(b, i, part):
                yield from idle(4)
                pool.wait_ge(*bank_read(b, ("var", i)))
                nc.gpsimd.tensor_tensor(RS[:, :], VE[:, :], POW[:, :], ALU.pow).then_inc(sems[part + "_rs"], 1)
                yield from idle(LN - 4)

            def val(b, has_post):
                yield from idle(VAL)

            def post(b, in_loop):
                yield from idle(HEAD)
                yield from ln(b, 2, "post")
                yield from idle(FF)
                yield from ln(b, 3, "post")

            def pre(b, has_post):
                yield from idle(2 * GAT)
                yield from ln(b, 0, "pre")
                yield from idle(FF)
                yield from ln(b, 1, "pre")
                yield from idle(QKV + SPLIT)

            def masks(b, t):
                if t == 0:
                    pool.wait_ge(*at("lm_ready", b, 0))
                    pool.wait_ge(*at("m1_in", b, 0))
                pool.wait_ge(*at(f"chunk_in{t % MAX_CHUNKS}", b, 16 * (t // MAX_CHUNKS + 1)))
                pool.sem_inc(chunk_there, 1)
                nc.gpsimd.tensor_scalar(NM[:, t, :], AC[:, t % MAX_CHUNKS, :], 0.0, FAR, ALU.is_le, ALU.mult)
                nc.gpsimd.tensor_scalar(M1S[:, t, :], AC[:, t % MAX_CHUNKS, :], 1.0, None, ALU.is_equal).then_inc(
                    sems["chunk_used"], 1)

            def main(b, has_post, has_pre):
                for _ in side_of((val, post, pre, masks), b, has_post, has_pre):
                    pass

            for _ in pre((0, 0), False):
                pass
            main((0, 0), False, True)
            with pool.Fori(0, B - 2) as c:
                main((c, 1), True, True)
            main((0, B - 1), True, False)
            for _ in post((0, B - 1), False):
                pass

        @block.scalar
        def _(act):
            act.sem_inc(sems["r_done"], 1)
            act.wait_ge(w_in, 16 * NW)
            act.wait_ge(dmade, 15)
            nc.scalar.mul(BQ4[:, :], col("bq"), 0.25).then_inc(made, 1)
            act.wait_ge(made, 1)
            for k, name in enumerate(("a1s", "a2s")):
                act.wait_ge(pmade, 11)
                nc.scalar.activation(AREP[:, k, :], ZERO, ACT.Identity, bias=col(name)).then_inc(made, 1)
            for k in range(2):
                act.wait_ge(prep_full, k + 1)
                nc.scalar.mul(WREP[:, k, :], st[k][:, 0, 0:P], -1.0).then_inc(made, 1)
                nc.scalar.mul(WX[:, k, P:P + 1], st[k][:, 1, 0:1], -0.8).then_inc(made, 1)
                nc.scalar.copy(WX[:, k, 0:P], gW[k]).then_inc(made, 1)

            def ln(b, i):
                yield
                for half in range(2):
                    key = ("xc", i, half)
                    act.wait_ge(*bank_full(b, key))
                    nc.scalar.copy(XC[:, half, :], bank(key)[:, :])
                    nc.scalar.activation(SQ[:, half, :], bank(key)[:, :], ACT.Square).then_inc(free(key), 1)
                    yield
                yield from idle(LN - 3)

            def ff(b, i, func, bias):
                for half in range(2):
                    yield
                    for c in range(HC):
                        key = ("f1", i, half, c)
                        act.wait_ge(*bank_full(b, key))
                        nc.scalar.activation(FA[:, c, :], bank(key)[:, :], func, bias=col(bias, c)).then_inc(free(key), 1)
                        yield from idle(1 if c == 0 else 2)
                    yield

            def keep_input(b, before):
                if before is not None:
                    act.wait_ge(*bank_read(before, ("wo", 1)))
                act.wait_ge(*at("pre_ln", b, 4))
                nc.scalar.copy(RES[:, :], X2[:, :]).then_inc(sems["res_ready"], 1)

            def val(b, has_post):
                if not has_post:
                    keep_input(b, None)
                yield from idle(VAL)

            def post(b, in_loop):
                yield from idle(2)
                act.wait_ge(*bank_read(b, ("sm",)))
                if in_loop:
                    act.wait_ge(*at("p3_ready", graph_of(b, 1), 2))
                for gi in range(4):
                    nc.scalar.copy(FA[:, gi, :].rearrange("p (a k) -> p a k", k=32),
                                   RCP[:, 4 * gi:4 * gi + 4, :].rearrange("p a (h o) -> p (a h) o", o=1)
                                   .to_broadcast([P, 16, 32])).then_inc(sems["rx_ready"], 1)
                    yield
                yield from idle(HEAD - 6)
                if in_loop:
                    keep_input(graph_of(b, 1), b)
                yield from ln(b, 2)
                yield from ff(b, 1, ACT.Gelu, "b1")
                yield from ln(b, 3)

            def seen(b, t):
                act.wait_ge(*at(f"chunk_in{t % MAX_CHUNKS}", b, 16 * (t // MAX_CHUNKS + 1)))
                if t >= 1 or not is_first(b):
                    act.wait_ge(*at("chunk_seen", b, t))
                nc.scalar.activation(SEEN[:, :], AC[:, t % MAX_CHUNKS, :], ACT.Square, bias=HALFN[:, :],
                                     accum_out=CHK[:, t:t + 1]).then_inc(sems["chunk_seen"], 1)

            def pre(b, has_post):
                for k in range(2):
                    yield
                    if k == 0 and not is_first(b):
                        act.wait_ge(*at("stack_in0", b, 0))
                        act.wait_ge(*at("stack_in1", b, 0))
                        if has_post:
                            act.wait_ge(*at("post_ln", graph_of(b, -2), 4))
                    for half in range(2):
                        key = ("s", k, half)
                        act.wait_ge(*bank_full(b, key))
                        nc.scalar.mul(SN2[:, hs(half)], bank(key)[:, :], 0.2).then_inc(sems["sn_ready"], 1)
                        nc.scalar.copy(SN[:, hs(half)], bank(key)[:, :]).then_inc(free(key), 1)
                        yield
                    for w in range(3):
                        key = ("wh", k, w)
                        act.wait_ge(*bank_full(b, key))
                        n = min(3, NT - 3 * w)
                        nc.scalar.copy(WH[:, 3 * w:3 * w + n, :],
                                       bank(key)[:, 0:n * (P + 1)].rearrange("p (t f) -> p t f", t=n)).then_inc(free(key), 1)
                        if w == 0:
                            yield
                    if k == 0 and not has_post:
                        seen(b, 0)
                    yield
                    for j in range(NT + 3):
                        if k == 0 and not has_post and j + 1 < NT:
                            seen(b, j + 1)
                        t = j - 1
                        if 0 <= t < NT:
                            act.wait_ge(*at("lm_ready", b, NT * k + t + 1))
                            if t >= 3:
                                act.wait_ge(*at("e_used", b, (NT - 1) * k + t - 2))
                            nc.scalar.activation(E[t % 3].rearrange("p a n -> p (a n)"), LP[t % 3], ACT.Exp, scale=-1.0,
                                                 bias=LMIN[:, t:t + 1], accum_out=ESUM[:, t:t + 1]).then_inc(sems["e_ready"], 1)
                        yield
                    if k == 0:
                        if not is_first(b):
                            act.wait_ge(*at("res_ready", b, 0))
                        for half in range(2):
                            key = ("gout", 0, half)
                            act.wait_ge(*bank_full(b, key))
                            nc.scalar.copy(H1[:, hs(half)], bank(key)[:, :]).then_inc(free(key), 1)
                    yield
                yield from ln(b, 0)
                yield from ff(b, 0, ACT.Relu, "bff1")
                yield from ln(b, 1)
                yield
                for w, half in ((0, 0), (0, 1), (1, 0), (1, 1)):
                    key = ("qk"[w], half)
                    act.wait_ge(*bank_full(b, key))
                    nc.scalar.activation(QK[:, w, hs(half)], bank(key)[:, :], ACT.Identity,
                                         bias=BQ4[:, :] if w == 0 else col("bk"),
                                         scale=0.25 if w == 0 else 1.0).then_inc(free(key), 1)
                    if (w, half) != (0, 0):
                        yield
                yield from idle(SPLIT)

            def maxima_out(b, g):
                act.wait_ge(*at("ct_full", b, g + 1))
                if g == 1:
                    act.wait_ge(*at("c_in", b, 16 * CROWS))
                elif not is_first(b):
                    act.wait_ge(*at("c_in", b, 0))
                nc.scalar.copy(CR[:, :], pv[:, :].bitcast(BF16)[0:CROWS * 4, :]).then_inc(sems["ct_read"], 1)

            def output_out(b, n, has_post):
                act.wait_ge(*at("p_used", b, n))
                gi = n // NT - 1
                if gi == 0 and has_post:
                    act.wait_ge(*bank_full(graph_of(b, -1), ("wo", 1)))
                nc.scalar.copy(U[:, gi, :], pv[:, :]).then_inc(sems["u_ready"], 1)

            def general_step(b, t, it, g, step):
                act.wait_ge(*at_step("r_done", step, 0))
                act.dma_start(AR, adj_t[b[0] + b[1], t, :, it, :]).then_inc(sems["r_adj"], 16)
                nc.scalar.copy(XB, RES[:, :].rearrange("p (t n) -> p t n", t=NT)[:, t, :]).then_inc(sems["r_xb"], 1)
                act.wait_ge(*at_step("r_st", step, 1))
                for pr in range(2):
                    ins = nc.scalar.activation(PT[:, 0, 2 * pr:2 * pr + 2, :], st[pr][:, :, :], ACT.Exp)
                ins.then_inc(sems["r_p"], 1)

            def main(b, has_post, has_pre):
                side = side_of((val, post, pre, seen), b, has_post, has_pre)
                for tick in range(MAX_TICKS):
                    if tick == MAX_TICKS // 2 + 3:
                        maxima_out(b, 0)
                    turn(side, tick)
                for n in range(ATT):
                    g = n // (2 * NT)
                    if n % (2 * NT) == 0 and (g == 1 or not is_first(b)):
                        act.wait_ge(*at("u_done", b, g))
                    for pr in range(2):
                        act.wait_ge(*at("st_full", b, 2 * n + pr + 1))
                        if pr == 0 and n % (2 * NT) >= 3:
                            act.wait_ge(*at("p_used", b, n - 2))
                        nc.scalar.activation(PT[:, n % 3, 2 * pr:2 * pr + 2, :], st[pr][:, :, :], ACT.Exp).then_inc(
                            sems["p_ready"], 1)
                    if n == 0:
                        maxima_out(b, 1)
                    next(side, None)
                    if n % (2 * NT) == NT:
                        output_out(b, n, has_post)
                    if n % (2 * NT) == 2 * NT - 1:
                        output_out(b, n + 1, has_post)
                        act.wait_ge(*at("flag_ready", b, 1))
                        act.sem_inc(flag_seen, 1)
                        flag = act.value_load(FLAG[0:1, 0:1], min_val=0, max_val=1)
                        with act.If(flag == 1):
                            with act.Fori(0, NT) as t:
                                with act.Fori(0, NHALF) as it:
                                    general_step(b, t, it, g, step_number(b, g, t, it))
                        with act.Else():
                            for name in ("r_adj", "r_xb", "r_p"):
                                act.sem_inc(sems[name], per[name] // 2)
                    turn(side, MAX_TICKS + n)
                for _ in side:
                    pass

            for _ in pre((0, 0), False):
                pass
            main((0, 0), False, True)
            with act.Fori(0, B - 2) as c:
                main((c, 1), True, True)
            main((0, B - 1), True, False)
            for _ in post((0, B - 1), False):
                pass

        @block.vector
        def _(dve):
            nc.vector.memset(WO[:, :, :], 0.0).then_inc(wo_zero, 1)
            nc.vector.memset(VV[:, :], 0.0).then_inc(dmade, 1)
            nc.vector.memset(KS[KROWS:P, :, :], 1.0).then_inc(dmade, 1)
            nc.vector.memset(VC[:, :, :, :], 0.0).then_inc(dmade, 1)
            nc.vector.memset(HALFN[:, :], -0.5).then_inc(dmade, 1)
            dve.wait_ge(dmade, 4)
            nc.vector.memset(V4[:, :, 0, :, DH:DH + 1], 1.0).then_inc(dmade, 1)
            dve.wait_ge(w_in, 16 * NW)
            nc.vector.tensor_copy(WV[:, 0, :], WVR[:, 0, :]).then_inc(dmade, 1)
            nc.vector.tensor_copy(BVD[:, 0, :], BV[:, 0, :]).then_inc(dmade, 1)
            nc.vector.tensor_tensor(WV[:, 1, :], WVR[:, 1, :], WVR[:, 0, :], ALU.subtract).then_inc(dmade, 1)
            nc.vector.tensor_tensor(BVD[:, 1, :], BV[:, 1, :], BV[:, 0, :], ALU.subtract).then_inc(dmade, 1)
            for dst, src in ((WVX, WVR), (BVX, BV)):
                for r in range(2):
                    nc.vector.tensor_tensor(dst[:, r, :], src[:, 2 + r, :], src[:, 0, :], ALU.subtract).then_inc(dmade, 1)
                nc.vector.tensor_scalar(dst[:, 2, :], src[:, 0, :], -1.0, None, ALU.mult).then_inc(dmade, 1)

            def ln(b, i, part, g, be, dst):
                yield from idle(4)
                key = ("var", i)
                dve.wait_ge(*bank_full(b, key))
                nc.vector.tensor_scalar(VE[:, :], bank(key)[:, 0:NT], EPS, None, ALU.add).then_inc(free(key), 1)
                yield from idle(2)
                for half in range(2):
                    key = ("bc", i, half)
                    dve.wait_ge(*bank_full(b, key))
                    nc.vector.scalar_tensor_tensor(out=XC[:, half, :], in0=XC[:, half, :], scalar=col(g),
                                                   in1=bank(key)[:, :], op0=ALU.mult, op1=ALU.mult).then_inc(free(key), 1)
                    yield
                for half in range(2):
                    dve.wait_ge(*bank_read(b, ("bc", i, half)))
                    nc.vector.tensor_scalar(dst[:, hs(half)], XC[:, half, :], col(be), None, ALU.add).then_inc(
                        sems[part + "_ln"], 1)
                yield

            def ff_out(b, i, bias, res):
                for half in range(2):
                    yield from idle(8)
                    key = ("f2", i, half)
                    dve.wait_ge(*bank_full(b, key))
                    nc.vector.scalar_tensor_tensor(out=YT[:, hs(half)], in0=bank(key)[:, :], scalar=col(bias),
                                                   in1=res[:, hs(half)], op0=ALU.add, op1=ALU.add).then_inc(free(key), 1)
                    yield

            def val(b, has_post):
                dve.wait_ge(*bank_read(b, ("fl",)))
                if has_post:
                    dve.wait_ge(*at("r_acc", b, 0))
                    dve.wait_ge(*at("r_p", b, 0))
                    dve.wait_ge(*at("p_used", b, 0))
                else:
                    dve.wait_ge(dmade, 15)
                nc.vector.tensor_scalar(FLAG[:, :], FMAX[:, :], N / 4.0, None, ALU.is_gt).then_inc(sems["flag_ready"], 1)
                yield
                for i in range(NT // 2):
                    key = ("v", i)
                    dve.wait_ge(*bank_full(b, key))
                    for j in range(2):
                        ins = nc.vector.tensor_tensor(
                            V4[:, 2 * i + j, :, :, 0:DH].rearrange("p w h d -> p (w h) d"),
                            bank(key)[:, 256 * j:256 * (j + 1)].rearrange("p (g d) -> p g d", d=DH),
                            BVD[:, :, :].rearrange("p w (h d) -> p (w h) d", d=DH), ALU.add)
                    ins.then_inc(free(key), 1)
                    yield

            def post(b, in_loop):
                yield
                key = ("sm",)
                dve.wait_ge(*bank_full(b, key))
                nc.vector.reciprocal(RCP[:, :, :].rearrange("p a h -> p (a h)"), bank(key)[:, 0:64]).then_inc(free(key), 1)
                yield from idle(3)
                for gi in range(4):
                    key = ("rb", gi)
                    dve.wait_ge(*bank_full(b, key))
                    nc.vector.tensor_tensor(U[:, gi, :], U[:, gi, :], bank(key)[:, :], ALU.mult).then_inc(free(key), 1)
                    yield
                yield
                for half in range(2):
                    key = ("wo", half)
                    dve.wait_ge(*bank_full(b, key))
                    if half == 0:
                        dve.wait_ge(*at("res_ready", b, 1))
                        if not in_loop:
                            dve.wait_ge(*at("out_done", b, 0))
                    nc.vector.scalar_tensor_tensor(out=YT[:, hs(half)], in0=bank(key)[:, :], scalar=col("bo"),
                                                   in1=RES[:, hs(half)], op0=ALU.add, op1=ALU.add).then_inc(free(key), 1)
                    yield
                yield from ln(b, 2, "post", "g1", "be1", HT)
                yield from ff_out(b, 1, "b2", HT)
                yield from ln(b, 3, "post", "g2", "be2", OT)

            def masks(b, t):
                dve.wait_ge(*at(f"chunk_in{t % MAX_CHUNKS}", b, 16 * (t // MAX_CHUNKS + 1)))
                nc.vector.tensor_scalar(NM[:, t, :], AC[:, t % MAX_CHUNKS, :], 0.0, FAR, ALU.is_le, ALU.mult)
                nc.vector.tensor_scalar(M1S[:, t, :], AC[:, t % MAX_CHUNKS, :], 1.0, None, ALU.is_equal).then_inc(
                    sems["chunk_used"], 1)

            def logits(b, k, t, has_post):
                if t == 0:
                    for half in range(2):
                        dve.wait_ge(*bank_read(b, ("s", k, half)))
                    if k == 0 and not is_first(b):
                        dve.wait_ge(*at("stack_in0", b, 0))
                        dve.wait_ge(*at("stack_in1", b, 0))
                        if has_post:
                            dve.wait_ge(*at("out_done", graph_of(b, -2), 16))
                if t % 3 == 0:
                    dve.wait_ge(*bank_read(b, ("wh", k, t // 3)))
                if t >= 3:
                    dve.wait_ge(*at("e_ready", b, NT * k + t - 2))
                nc.vector.scalar_tensor_tensor(out=LP[t % 3], in0=SN, scalar=WH[:, t, P:P + 1],
                                               in1=SN2, op0=ALU.add, op1=ALU.min).then_inc(sems["lp_ready"], 1)

            def masked(b, k, t):
                if k == 0:
                    dve.wait_ge(*at("chunk_used", b, t + 1))
                dve.wait_ge(*at("lp_ready", b, NT * k + t + 1))
                dve.sem_inc(lp_seen, 1)
                nc.vector.tensor_tensor_reduce(out=LP[t % 3], in0=LP[t % 3], in1=NM[:, t, :],
                                               scale=1.0, scalar=3e38, op0=ALU.add, op1=ALU.min,
                                               accum_out=LMIN[:, t:t + 1]).then_inc(sems["lm_ready"], 1)

            def norm(b, k, t):
                dve.wait_ge(*at("e_ready", b, NT * k + t + 1))
                nc.vector.reciprocal(ERCP[:, t:t + 1], ESUM[:, t:t + 1]).then_inc(sems["rcp_ready"], 1)
                dve.wait_ge(*at("rcp_ready", b, NT * k + t + 1))
                if t >= 4:
                    dve.wait_ge(*at("e_used", b, (NT - 1) * k + t - 3))
                nc.vector.tensor_scalar(WHS[:, t % 4, :], WH[:, t, 0:P], ERCP[:, t:t + 1], None, ALU.mult).then_inc(
                    sems["whs_ready"], 1)

            def pre(b, has_post):
                for k in range(2):
                    yield from idle(4)
                    if k == 0 and not has_post:
                        if not is_first(b):
                            dve.wait_ge(*at("lm_ready", b, 0))
                            dve.wait_ge(*at("m1_in", b, 0))
                        masks(b, 0)
                    yield
                    logits(b, k, 0, has_post)
                    for j in range(NT + 3):
                        if k == 0 and not has_post and j + 1 < NT:
                            masks(b, j + 1)
                        if j + 1 < NT:
                            logits(b, k, j + 1, has_post)
                        if j < NT:
                            masked(b, k, j)
                        if 0 <= j - 2 < NT:
                            norm(b, k, j - 2)
                        yield
                    if k == 1:
                        for half in range(2):
                            key = ("gout", 1, half)
                            dve.wait_ge(*bank_full(b, key))
                            if half == 0:
                                dve.wait_ge(*at("x_in", b, 16))
                            nc.vector.tensor_tensor(YT[:, hs(half)], bank(key)[:, :], XT[:, hs(half)], ALU.add).then_inc(free(key), 1)
                    yield
                key = ("fl",)
                dve.wait_ge(*bank_full(b, key))
                nc.vector.reduce_max(FMAX[:, :], bank(key)[:, 0:NT], AX.X).then_inc(free(key), 1)
                yield from ln(b, 0, "pre", "gln1", "bln1", HT)
                yield from ff_out(b, 0, "bff2", HT)
                yield from ln(b, 1, "pre", "gln2", "bln2", X2)
                yield from idle(QKV)
                for w in range(2):
                    for half in range(2):
                        dve.wait_ge(*bank_read(b, ("qk"[w], half)))
                    nc.vector.tensor_copy(QP[:, w, 0, :], QK[:, w, :]).then_inc(sems["p1_ready"], 1)
                    yield
                for w in range(2):
                    dve.wait_ge(*at("p1_ready", b, w + 1))
                    nc.vector.tensor_tensor(QK[:, w, :], QK[:, w, :], QP[:, w, 0, :], ALU.subtract).then_inc(sems["r1_ready"], 1)
                    yield
                for w in range(2):
                    dve.wait_ge(*at("r1_ready", b, w + 1))
                    nc.vector.tensor_copy(QP[:, w, 1, :], QK[:, w, :]).then_inc(sems["p2_ready"], 1)
                    yield
                for w in range(2):
                    dve.wait_ge(*at("p2_ready", b, w + 1))
                    nc.vector.tensor_tensor(QP[:, w, 2, :], QK[:, w, :], QP[:, w, 1, :], ALU.subtract).then_inc(sems["p3_ready"], 1)
                    yield

            def pieces_of_maxima(b, g):
                dve.wait_ge(*at("mx_read", b, 4 * NT * (g + 1)))
                nc.vector.tensor_scalar(MNEG[:, g], MX[:, g], -1.0, None, ALU.mult).then_inc(sems["mneg_ready"], 1)
                dve.wait_ge(*at("mneg_ready", b, g + 1))
                nc.vector.tensor_copy(CM[:, g, :, 0, :], MNEG[:, g]).then_inc(sems["c1_ready"], 1)
                dve.wait_ge(*at("c1_ready", b, g + 1))
                nc.vector.tensor_tensor(MR[:, g], MNEG[:, g], CM[:, g, :, 0, :], ALU.subtract).then_inc(sems["mr_ready"], 1)
                dve.wait_ge(*at("mr_ready", b, g + 1))
                nc.vector.tensor_copy(CM[:, g, :, 1, :], MR[:, g]).then_inc(sems["c2_ready"], 1)
                dve.wait_ge(*at("c2_ready", b, g + 1))
                nc.vector.tensor_tensor(CM[:, g, :, 2, :], MR[:, g], CM[:, g, :, 1, :], ALU.subtract).then_inc(sems["cm_ready"], 1)

            def general_step(t, it, g, step):
                dve.wait_ge(*at_step("r_done", step, 0))
                dve.wait_ge(*at_step("r_v", step, 1))
                vx = pv[:, 0:3 * P].rearrange("p (r g f) -> p r g f", r=3, g=2)
                bx = BVX[:, :, :].rearrange("p r (g f) -> p r g f", g=2)
                for r in range(3):
                    ins = nc.vector.tensor_tensor(VC[:, r, :, 0:DH], vx[:, r, g, :].rearrange("p (h d) -> p h d", d=DH),
                                                  bx[:, r, g, :].rearrange("p (h d) -> p h d", d=DH), ALU.add)
                ins.then_inc(sems["r_vc"], 1)
                dve.wait_ge(*at_step("r_adj", step, 16))
                nc.vector.tensor_scalar(BELOW, AR, 0.0, None, ALU.is_lt).then_inc(sems["r_below"], 1)
                nc.vector.tensor_scalar(MK[:, 0, :], AR, 2.0, None, ALU.is_equal)
                nc.vector.tensor_scalar(MK[:, 1, :], AR, 3.0, None, ALU.is_equal)
                dve.wait_ge(*at_step("r_below", step, 1))
                nc.vector.scalar_tensor_tensor(out=MK[:, 2, :], in0=AR, scalar=3.0, in1=BELOW,
                                               op0=ALU.is_gt, op1=ALU.add).then_inc(sems["r_mask"], 1)
                dve.wait_ge(*at_step("r_mask", step, 1))
                dve.wait_ge(*at_step("r_p", step, 1))
                for r in range(3):
                    if r == 2:
                        dve.wait_ge(*at_step("r_acc", step, 1))
                    nc.vector.tensor_tensor(PM[:, r % 2, :, :], PT[:, 0, :, :],
                                            MK[:, r:r + 1, :].to_broadcast([P, 4, HALF]), ALU.mult).then_inc(sems["r_pm"], 1)
                dve.wait_ge(*at_step("r_acc", step, 3))
                u = U[:, :, :].rearrange("p (g i) n -> p g i n", g=2)[:, g, it, :]
                nc.vector.tensor_tensor(u, u, pv[:, :], ALU.add).then_inc(sems["r_done"], 1)

            def main(b, has_post, has_pre):
                side = side_of((val, post, pre), b, has_post, has_pre)
                for tick in range(MAX_TICKS):
                    g, h, t = tick // (4 * NT), tick // NT % 4, tick % NT
                    dve.wait_ge(*at("mx_full", b, tick + 1))
                    nc.vector.reduce_max(MX[:, g, t, h:h + 1], st[tick % 2][:, :, :].rearrange("p a n -> p (a n)"),
                                         AX.X).then_inc(sems["mx_read"], 1)
                    if tick % (4 * NT) == 4 * NT - 1:
                        pieces_of_maxima(b, g)
                    turn(side, tick)
                dve.wait_ge(*at("m1_in", b, 16))
                for n in range(ATT):
                    g, it, t = n // (NHALF * NT), n // NT % NHALF, n % NT
                    for pr in range(2):
                        dve.wait_ge(*at("p_ready", b, 2 * n + pr + 1))
                        if pr == 0 and n % (2 * NT) >= 2:
                            dve.wait_ge(*at("p_used", b, n - 1))
                        nc.vector.tensor_tensor(
                            PM[:, n % 2, 2 * pr:2 * pr + 2, :], PT[:, n % 3, 2 * pr:2 * pr + 2, :],
                            M1[:, t:t + 1, hs(it)].to_broadcast([P, 2, HALF]), ALU.mult).then_inc(sems["pm_ready"], 1)
                        if pr == 0:
                            next(side, None)
                    if n % (2 * NT) == 2 * NT - 1:
                        dve.wait_ge(*at("u_ready", b, 2 * g + 2))
                        dve.wait_ge(*at("flag_ready", b, 1))
                        dve.sem_inc(flag_seen, 1)
                        flag = dve.value_load(FLAG[0:1, 0:1], min_val=0, max_val=1)
                        with dve.If(flag == 1):
                            with dve.Fori(0, NT) as tt:
                                with dve.Fori(0, NHALF) as ii:
                                    general_step(tt, ii, g, step_number(b, g, tt, ii))
                        with dve.Else():
                            for name in ("r_vc", "r_below", "r_mask", "r_pm", "r_done"):
                                dve.sem_inc(sems[name], per[name] // 2)
                        dve.wait_ge(*at("r_done", b, STEPS // 2 * (g + 1)))
                        dve.sem_inc(sems["u_done"], 1)
                    turn(side, MAX_TICKS + n)
                for _ in side:
                    pass

            for _ in pre((0, 0), False):
                pass
            main((0, 0), False, True)
            with dve.Fori(0, B - 2) as c:
                main((c, 1), True, True)
            main((0, B - 1), True, False)
            for _ in post((0, B - 1), False):
                pass

        @block.tensor
        def _(pe):
            pe.wait_ge(w_in, 16 * NW)
            pe.wait_ge(pmade, 11)
            pe.wait_ge(dmade, 15)
            for k in range(2):
                pe.wait_ge(made, 3)
                nc.tensor.matmul(st[k][:, 0, 0:P], gWT[k], AREP[:, k, :], start=True, stop=True)
                nc.tensor.matmul(st[k][:, 1, 0:1], gWT[k], col(("a1t", "a2t")[k]), start=True, stop=True).then_inc(prep_full, 1)
            pe.wait_ge(made, 9)

            def part_begins(b, part):
                for i in range(3):
                    pe.wait_ge(*at(f"{part}_free{i}", b, used[part][i]))

            def ln(b, i, part, made_by):
                for half in range(2):
                    key = ("xc", i, half)
                    pe.wait_ge(*bank_read(b, made_by(half)))
                    if not first_use(key):
                        pe.wait_ge(*bank_idle(b, key))
                    nc.tensor.matmul(bank(key)[:, :], CEN[:, :], YT[:, hs(half)], start=True, stop=True).then_inc(full(key), 1)
                    yield
                yield
                pe.wait_ge(*bank_read(b, ("xc", i, 0)))
                pe.wait_ge(*bank_read(b, ("xc", i, 1)))
                key = ("var", i)
                pe.wait_ge(*bank_idle(b, key))
                for t in range(NT):
                    ins = nc.tensor.matmul(bank(key)[:, t:t + 1], SQ[:, t // 4, t % 4 * P:(t % 4 + 1) * P], MEAN[:, 0:1],
                                           start=True, stop=True)
                ins.then_inc(full(key), 1)
                yield from idle(2)
                pe.wait_ge(*at(part + "_rs", b, i % 2 + 1))
                for half in range(2):
                    key = ("bc", i, half)
                    pe.wait_ge(*bank_idle(b, key))
                    for c in range(4):
                        t = 4 * half + c
                        ins = nc.tensor.transpose(bank(key)[:, c * P:(c + 1) * P], RS[:, t:t + 1].to_broadcast([P, P]),
                                                  IDF[:, :])
                    ins.then_inc(full(key), 1)
                    yield
                yield from idle(2)

            def ff(b, i, part, src, w1, w2):
                def up(half, c):
                    key = ("f1", i, half, c)
                    pe.wait_ge(*bank_idle(b, key))
                    nc.tensor.matmul(bank(key)[:, :], w1[:, c * P:(c + 1) * P], src[:, hs(half)],
                                     start=True, stop=True).then_inc(full(key), 1)

                def down(half, c):
                    key = ("f2", i, half)
                    pe.wait_ge(*bank_read(b, ("f1", i, half, c)))
                    if c == 0:
                        pe.wait_ge(*bank_idle(b, key))
                    ins = nc.tensor.matmul(bank(key)[:, :], w2[:, c, :], FA[:, c, :], start=(c == 0), stop=(c == HC - 1))
                    if c == HC - 1:
                        ins.then_inc(full(key), 1)

                for half in range(2):
                    pe.wait_ge(*at(part + "_ln", b, 2))
                    up(half, 0)
                    yield
                    up(half, 1)
                    yield
                    for c in range(HC):
                        down(half, c)
                        yield
                        if c + 2 < HC:
                            up(half, c + 2)
                            yield
                    yield

            def val(b, has_post):
                part_begins(b, "pre")
                pe.wait_ge(*at("pre_ln", b, 4))
                for i in range(NT // 2):
                    key = ("v", i)
                    if not first_use(key):
                        pe.wait_ge(*bank_idle(b, key))
                    for j in range(2):
                        t = 2 * i + j
                        ins = nc.tensor.matmul(bank(key)[:, 256 * j:256 * (j + 1)], X2[:, t * P:(t + 1) * P],
                                               WV[:, :, :].rearrange("p w f -> p (w f)"), start=True, stop=True)
                    ins.then_inc(full(key), 1)
                    yield
                yield

            def post(b, in_loop):
                if in_loop:
                    part_begins(graph_of(b, 1), "val")
                else:
                    part_begins(graph_of(b, -1), "post")
                pe.wait_ge(*at("u_done", b, 2))
                key = ("sm",)
                for a in range(16):
                    ins = nc.tensor.matmul(bank(key)[:, 4 * a:4 * a + 4], U[:, a // 4, a % 4 * P:(a % 4 + 1) * P], SEL[:, :],
                                           start=True, stop=True)
                ins.then_inc(full(key), 1)
                yield from idle(3)
                for gi in range(4):
                    key = ("rb", gi)
                    pe.wait_ge(*at("rx_ready", b, gi + 1))
                    if not first_use(key):
                        pe.wait_ge(*bank_idle(b, key))
                    for c in range(4):
                        ins = nc.tensor.transpose(bank(key)[:, c * P:(c + 1) * P], FA[:, gi, c * P:(c + 1) * P], IDF[:, :])
                    ins.then_inc(full(key), 1)
                    yield
                yield
                for gi in range(4):
                    pe.wait_ge(*bank_read(b, ("rb", gi)))
                for half in range(2):
                    key = ("wo", half)
                    pe.wait_ge(*bank_idle(b, key))
                    for g in range(2):
                        ins = nc.tensor.matmul(bank(key)[:, :], WO[:, g, :], U[:, 2 * g + half, :], start=(g == 0), stop=(g == 1))
                    ins.then_inc(full(key), 1)
                    yield
                yield
                yield from ln(b, 2, "post", lambda half: ("wo", half))
                yield from ff(b, 1, "post", HT, W1, W2)
                yield from ln(b, 3, "post", lambda half: ("f2", 1, half))

            def pre(b, has_post):
                if has_post:
                    part_begins(graph_of(b, -2), "post")
                elif not is_first(b):
                    part_begins(graph_of(b, -1), "val")
                for k in range(2):
                    h = (XT, H1)[k]
                    if k == 0:
                        pe.wait_ge(*at("x_in", b, 16))
                    else:
                        for half in range(2):
                            pe.wait_ge(*bank_read(b, ("gout", 0, half)))
                    for half in range(2):
                        key = ("s", k, half)
                        if not first_use(key):
                            pe.wait_ge(*bank_idle(b, key))
                        nc.tensor.matmul(bank(key)[:, :], WREP[:, k, :], h[:, hs(half)], start=True, stop=True).then_inc(full(key), 1)
                    yield
                    for w in range(3):
                        key = ("wh", k, w)
                        if not first_use(key):
                            pe.wait_ge(*bank_idle(b, key))
                        for j in range(min(3, NT - 3 * w)):
                            t = 3 * w + j
                            ins = nc.tensor.matmul(bank(key)[:, j * (P + 1):(j + 1) * (P + 1)], h[:, t * P:(t + 1) * P],
                                                   WX[:, k, :], start=True, stop=True)
                        ins.then_inc(full(key), 1)
                        yield
                    yield
                    yield from idle(3)
                    for t in range(NT):
                        pe.wait_ge(*at("whs_ready", b, NT * k + t + 1))
                        for half in range(2):
                            key = ("gout", k, half)
                            if t == 0:
                                pe.wait_ge(*bank_idle(b, key))
                            ins = nc.tensor.matmul(bank(key)[:, :], WHS[:, t % 4, :], E[t % 3][:, half, :],
                                                   start=(t == 0), stop=(t == NT - 1))
                            if t == NT - 1:
                                ins.then_inc(full(key), 1)
                        if t < NT - 1:
                            ins.then_inc(sems["e_used"], 1)
                        yield
                    yield
                pe.wait_ge(*at("chunk_seen", b, NT))
                key = ("fl",)
                pe.wait_ge(*bank_idle(b, key))
                nc.tensor.matmul(bank(key)[:, 0:NT], MEAN[:, :], CHK[:, :], start=True, stop=True).then_inc(full(key), 1)
                yield from ln(b, 0, "pre", lambda half: ("gout", 1, half))
                yield from ff(b, 0, "pre", HT, wff1, wff2)
                yield from ln(b, 1, "pre", lambda half: ("f2", 0, half))
                pe.wait_ge(*at("pre_ln", b, 4))
                for w, half in ((0, 0), (0, 1), (1, 0), (1, 1)):
                    key = ("qk"[w], half)
                    pe.wait_ge(*bank_idle(b, key))
                    nc.tensor.matmul(bank(key)[:, :], (Wq, Wk)[w], X2[:, hs(half)], start=True, stop=True).then_inc(full(key), 1)
                    if (w, half) != (0, 0):
                        yield
                yield from idle(1 + SPLIT)

            def whole_scores(b, tick, has_post):
                h, t = tick // NT, tick % NT
                if tick % (4 * NT) == 0:
                    pe.wait_ge(*at(f"stack_in{h // 4}", b, 16 * 2 * len(QK_PIECES)))
                if tick >= 2:
                    pe.wait_ge(*at("mx_read", b, tick - 1))
                elif has_post:
                    pe.wait_ge(*at("p_ready", b, 0))
                for half in range(2):
                    ins = nc.tensor.matmul(st[tick % 2][:, half, :], QS[0:KROWS, h, t * P:(t + 1) * P],
                                           KS[0:KROWS, h, hs(half)], start=True, stop=True)
                ins.then_inc(sems["mx_full"], 1)

            def transposed_maxima(b, g, has_post):
                pe.wait_ge(*at("cm_ready", b, g + 1))
                if g == 1:
                    pe.wait_ge(*at("ct_read", b, 1))
                elif has_post:
                    pe.wait_ge(*at("u_done", b, 0))
                for t in range(NT):
                    ins = nc.tensor.transpose(pv[:, :].bitcast(BF16)[0:CROWS * 4, t * P:(t + 1) * P],
                                              CM[:, g, t, :, :].rearrange("p c h -> p (c h)"), IDB[:, :])
                ins.then_inc(sems["ct_full"], 1)

            def scores(b, n):
                g, it, t = n // (NHALF * NT), n // NT % NHALF, n % NT
                if n % (2 * NT) == 0:
                    pe.wait_ge(*at("c_in", b, 16 * CROWS * (g + 1)))
                for pr in range(2):
                    if n >= 1:
                        pe.wait_ge(*at("p_ready", b, 2 * (n - 1) + pr + 1))
                    else:
                        pe.wait_ge(*at("mx_read", b, MAX_TICKS - 1 + pr))
                    for x in range(2):
                        h = 4 * g + 2 * pr + x
                        ins = nc.tensor.matmul(st[pr][:, x, :], KS[0:SROWS, h, t * P:(t + 1) * P],
                                               QS[0:SROWS, h, hs(it)], start=True, stop=True)
                    ins.then_inc(sems["st_full"], 1)

            def products(n, w, exps):
                g, t = n // (NHALF * NT), n % NT
                for x in range(4):
                    ins = nc.tensor.matmul(pv[32 * x:32 * x + 32, :], v_of(t, w, 4 * g + x), exps[:, x, :],
                                           start=(t == 0 and w == 0), stop=(t == NT - 1 and w == 1))
                return ins

            def gather(b, n):
                gi, t = n // NT, n % NT
                if n == 0:
                    pe.wait_ge(*at("ct_read", b, 2))
                elif n == 2 * NT:
                    pe.wait_ge(*at("u_done", b, 1))
                elif t == 0:
                    pe.wait_ge(*at("u_ready", b, gi))
                pe.wait_ge(*at("p_ready", b, 2 * n + 2))
                products(n, 0, PT[:, n % 3])
                pe.wait_ge(*at("pm_ready", b, 2 * n + 2))
                products(n, 1, PM[:, n % 2]).then_inc(sems["p_used"], 1)

            def general_step(g, t, it, step):
                pe.wait_ge(*at_step("r_xb", step, 1))
                nc.tensor.matmul(pv[:, 0:3 * P], XB, WVX[:, :, :].rearrange("p r f -> p (r f)"),
                                 start=True, stop=True).then_inc(sems["r_v"], 1)
                for x in range(4):
                    ins = nc.tensor.matmul(
                        st[x // 2][:, x % 2, :],
                        KS[:, :, :].rearrange("p h (t n) -> p h t n", t=NT)[0:SROWS, 4 * g + x, t, :],
                        QS[:, :, :].rearrange("p h (i n) -> p h i n", i=NHALF)[0:SROWS, 4 * g + x, it, :],
                        start=True, stop=True)
                ins.then_inc(sems["r_st"], 1)
                pe.wait_ge(*at_step("r_vc", step, 1))
                for r in range(3):
                    pe.wait_ge(*at_step("r_pm", step, r + 1))
                    for x in range(4):
                        ins = nc.tensor.matmul(pv[32 * x:32 * x + 32, :], VC[:, r, x, :], PM[:, r % 2, x, :],
                                               start=(r == 0), stop=(r == 2))
                    ins.then_inc(sems["r_acc"], 1)

            def main(b, has_post, has_pre):
                side = side_of((val, post, pre), b, has_post, has_pre)
                whole_scores(b, 0, has_post)
                for tick in range(MAX_TICKS):
                    if tick + 1 < MAX_TICKS:
                        whole_scores(b, tick + 1, has_post)
                    if tick == MAX_TICKS // 2 + 2:
                        transposed_maxima(b, 0, has_post)
                    turn(side, tick)
                for n in range(ATT):
                    if n % (2 * NT) == 0:
                        scores(b, n)
                        if n == 0:
                            transposed_maxima(b, 1, has_post)
                    if n % (2 * NT) != 0:
                        gather(b, n - 1)
                    next(side, None)
                    if (n + 1) % (2 * NT) != 0:
                        scores(b, n + 1)
                    else:
                        gather(b, n)
                        g = n // (2 * NT)
                        pe.wait_ge(*at("u_ready", b, 2 * g + 2))
                        pe.wait_ge(*at("flag_ready", b, 1))
                        pe.sem_inc(flag_seen, 1)
                        flag = pe.value_load(FLAG[0:1, 0:1], min_val=0, max_val=1)
                        with pe.If(flag == 1):
                            with pe.Fori(0, NT) as tt:
                                with pe.Fori(0, NHALF) as ii:
                                    general_step(g, tt, ii, step_number(b, g, tt, ii))
                        with pe.Else():
                            for name in ("r_v", "r_st", "r_acc"):
                                pe.sem_inc(sems[name], per[name] // 2)
                    turn(side, MAX_TICKS + n)
                for _ in side:
                    pass

            for _ in pre((0, 0), False):
                pass
            main((0, 0), False, True)
            with pe.Fori(0, B - 2) as c:
                main((c, 1), True, True)
            main((0, B - 1), True, False)
            for _ in post((0, B - 1), False):
                pass


def kernel(**inputs):
    import numpy as np
    import concourse.bacc as bacc
    from concourse.bass_utils import run_bass_kernel_spmd as run

    a = {k: np.asarray(v) for k, v in inputs.items()}

    def chunks(w):
        return w.reshape(HC, P, F).transpose(1, 0, 2).reshape(P, HC * F)

    def by_dim(w):
        return w.reshape(-1, 2, NH // 2, DH).transpose(0, 1, 3, 2).reshape(-1, F)

    def column(v):
        return v.reshape(-1, P).T

    g1, g2 = a["L0_gnn_W1"], a["L0_gnn_W2"]
    a1, a2 = a["L0_gnn_a1"].reshape(2, F), a["L0_gnn_a2"].reshape(2, F)
    arrays = {
        "xT": a["x"].transpose(0, 2, 1),
        "adjT": a["adj"].transpose(0, 2, 1),
        "mats": np.concatenate([g1, g2, g1.T, g2.T, a["L0_gnn_w_ff1"], chunks(a["L0_gnn_w_ff2"]),
                                by_dim(a["L1_gnn_Wq"]), by_dim(a["L1_gnn_Wk"]),
                                a["L1_gnn_W1"], chunks(a["L1_gnn_W2"])], axis=1),
        "wv": a["L1_gnn_Wv"].transpose(1, 0, 2),
        "wo": a["L1_gnn_Wo"],
        "cols": np.concatenate([column(v) for v in (
            a["L0_gnn_b_ff1"], a["L0_gnn_b_ff2"], a["L0_gnn_g_ln1"], a["L0_gnn_b_ln1"], a["L0_gnn_g_ln2"],
            a["L0_gnn_b_ln2"], by_dim(a["L1_gnn_bq"]), by_dim(a["L1_gnn_bk"]), a["L1_gnn_bo"], a["L1_gnn_b1"],
            a["L1_gnn_b2"], a["L1_gnn_g1"], a["L1_gnn_beta1"], a["L1_gnn_g2"], a["L1_gnn_beta2"],
            a1[0], a1[1], a2[0], a2[1])], axis=1),
        "bv": a["L1_gnn_bv"],
    }
    nc = bacc.Bacc("TRN2", target_bir_lowering=False, num_devices=1)
    given, args = {}, []
    for name, v in arrays.items():
        v = np.ascontiguousarray(v)
        given["in_" + name] = v
        args.append(nc.dram_tensor("in_" + name, v.shape, mybir.dt.from_np(v.dtype), kind="ExternalInput").ap())
    args.append(nc.dram_tensor("out_T", (B, F, N), F32, kind="ExternalOutput").ap())
    build(nc, *args)
    r = run(nc, [given], core_ids=[0])
    return np.ascontiguousarray(r.results[0]["out_T"].transpose(0, 2, 1))
```

```python
import concourse.bass as bass
from concourse import mybir
from contextlib import ExitStack

F32 = mybir.dt.float32
BF16 = mybir.dt.bfloat16
I32 = mybir.dt.int32
U8 = mybir.dt.uint8
ALU = mybir.AluOpType
ACT = mybir.ActivationFunctionType
AX = mybir.AxisListType

P = 128
B, N, F = 8, 1024, 128
HID = 512
NH, DH = 8, 16
VW = DH + 1
NT = N // P
HALF = 512
NHALF = N // HALF
HC = HID // P
EPS = 1e-5
FAR = 2.0 ** 100
QK_PIECES = [(0, 0), (0, 1), (1, 0), (1, 1), (0, 2), (2, 0)]
KROWS = 16 * len(QK_PIECES)
CROWS = 3
SROWS = KROWS + CROWS
STEPS = NT * NHALF * 2

COLS = {}
for _name, _n in (("bff1", HC), ("bff2", 1), ("gln1", 1), ("bln1", 1), ("gln2", 1), ("bln2", 1),
                  ("bq", 1), ("bk", 1), ("bo", 1), ("b1", HC), ("b2", 1),
                  ("g1", 1), ("be1", 1), ("g2", 1), ("be2", 1),
                  ("a1s", 1), ("a1t", 1), ("a2s", 1), ("a2t", 1)):
    COLS[_name] = (sum(n for _, n in COLS.values()), _n)
NCOLS = sum(n for _, n in COLS.values())


def bank_plan():
    def ln(i):
        return [("xc", i, 0), ("xc", i, 1), ("var", i), ("bc", i, 0), ("bc", i, 1)]

    def ff(i):
        return [key for half in range(2) for key in [("f1", i, half, c) for c in range(2)] + [("f2", i, half)]
                + [("f1", i, half, c) for c in range(2, HC)]]

    gat = []
    for k in range(2):
        gat += [("s", k, i) for i in range(2)] + [("wh", k, i) for i in range(3)]
        gat += [("gout", k, i) for i in range(2)]
    pre = ln(0) + ff(0) + ln(1) + [(w, half) for w in "qk" for half in range(2)]
    post = [("sm",)] + [("rb", gi) for gi in range(4)] + [("wo", half) for half in range(2)] + ln(2) + ff(1) + ln(3)
    values = [("v", i) for i in range(NT // 2)]
    plan, used = {}, {}
    for part, keys in (("gat", gat), ("pre", pre), ("val", values), ("post", post)):
        used[part] = [0, 0]
        for n, key in enumerate(keys):
            bank = {"f1": 0, "f2": 1}.get(key[0], n % 2)
            plan[key] = (part, bank, used[part][bank])
            used[part][bank] += 1
    return plan, used


def build(nc, xT, adjT, gwt, mats, wv, wo, cols, bv, outT):
    nc.disable_value_cache = True
    ctx = ExitStack()
    with ctx:
        def sb(name, shape, dt=F32):
            return ctx.enter_context(nc.sbuf_tensor(name, shape, dt))

        def ps(name, shape, dt=F32):
            return ctx.enter_context(nc.psum_tensor(name, shape, dt))

        MAT = sb("MAT", [P, mats.shape[1]])
        off = [0]

        def mat(width):
            off[0] += width
            return MAT[:, off[0] - width:off[0]]

        gW = [mat(P), mat(P)]
        wff1 = mat(HID)
        wff2 = mat(HID).rearrange("p (c f) -> p c f", c=HC)
        Wq = mat(P)
        Wk = mat(P)
        W1 = mat(HID)
        W2 = mat(HID).rearrange("p (c f) -> p c f", c=HC)
        WV = sb("WV", [P, 2, P])
        WO = sb("WO", [P, 2, P])
        COL = sb("COL", [P, NCOLS])
        BQ4 = sb("BQ4", [P, 1])
        BVD = sb("BVD", [P, 2, P])
        WREP = sb("WREP", [P, 2, P])
        WX = sb("WX", [P, 2, P + 1])
        CEN = sb("CEN", [P, P])
        MEAN = sb("MEAN", [P, P])
        SEL = sb("SEL", [P, 4])
        IDF = sb("IDF", [P, P])
        POW = sb("POW", [P, NT])
        IDB = sb("IDB", [P, P], BF16)
        HALFN = sb("HALFN", [P, 1])
        WVX = sb("WVX", [P, 3, P])
        BVX = sb("BVX", [P, 3, P])

        def col(name, c=0):
            return COL[:, COLS[name][0] + c:COLS[name][0] + c + 1]

        QS = sb("QS", [P, NH, N], BF16)
        KS = sb("KS", [P, NH, N], BF16)
        VV = sb("VV", [P, NT * 2 * NH * VW + 32])
        V4 = VV[:, 0:NT * 2 * NH * VW].rearrange("p (t w h d) -> p t w h d", t=NT, w=2, h=NH)
        M1 = sb("M1", [P, NT, N], U8)
        MX = sb("MX", [P, 2, NT, 4])
        MNEG = sb("MNEG", [P, 2, NT, 4])
        MR = sb("MR", [P, 2, NT, 4])
        CM = sb("CM", [P, 2, NT, CROWS, 4], BF16)
        CR = sb("CR", [CROWS * 4, N], BF16)
        PT = sb("PT", [P, 3, 4, HALF])
        PM = sb("PM", [P, 2, 4, HALF])
        U = sb("U", [P, 4, HALF])
        RES = sb("RES", [P, N])
        FLAG = sb("FLAG", [P, 1], I32)
        VC = sb("VC", [P, 3, 4, 32])
        XB = PT[:, 2, 1, 0:P]
        AR = PT[:, 2, 0, :].bitcast(I32)
        MK, BELOW = PT[:, 1, 0:3, :], PT[:, 1, 3, :]
        GWT = PT[:, 1, 0, 0:2 * P].rearrange("p (k f) -> p k f", k=2)
        WVR = PT[:, 0, 0, :].rearrange("p (r f) -> p r f", r=4)
        BV = PT[:, 0, 1, :].rearrange("p (r f) -> p r f", r=4)
        AREP = PT[:, 0, 2, 0:2 * P].rearrange("p (k f) -> p k f", k=2)
        ZERO = PT[:, 0, 3, 0:P]

        XT = sb("XT", [P, N])
        AM = sb("AM", [P, N], I32)
        AN = sb("AN", [P, N], I32)
        NM = sb("NM", [P, NT, N], BF16)
        WH = sb("WH", [P, NT, P + 1])
        WHS = sb("WHS", [P, 4, P])
        LMIN = sb("LMIN", [P, NT])
        ESUM = sb("ESUM", [P, NT])
        ERCP = sb("ERCP", [P, NT])
        LP = [sb(f"LP{i}", [P, 2, HALF]) for i in range(5)]
        SN = sb("SN", [P, N])
        SN2 = sb("SN2", [P, N])
        H1 = sb("H1", [P, N])
        X2 = sb("X2", [P, N])
        QP = sb("QP", [P, 2, 3, N], BF16)
        RCP = sb("RCP", [P, 16, 4])
        CHK = sb("CHK", [P, NT])
        FMAX = sb("FMAX", [P, 1])
        AREAS = {}
        for part, hidden, io in (("post", PM[:, 0, :, :], PM[:, 1, :, :]), ("pre", PT[:, 1, :, :], PT[:, 2, :, :])):
            small = PT[:, 0, 1 + len(AREAS), :]
            AREAS[part] = (
                hidden,
                hidden[:, 0:2, :], hidden[:, 2:4, :],
                io[:, 0:2, :].rearrange("p a n -> p (a n)"),
                io[:, 2:4, :].rearrange("p a n -> p (a n)"),
                small[:, 0:NT],
                small[:, NT:2 * NT],
            )
        QK = AREAS["pre"][0].rearrange("p (w a) n -> p w (a n)", w=2)
        OT = AREAS["post"][3]
        SEEN = PT[:, 0, 0, :].bitcast(BF16)

        ms = [ps(f"ms{i}", [P, HALF]) for i in range(3)]
        pv = ps("pv", [P, HALF])
        st = [ps(f"st{i}", [P, 2, HALF]) for i in range(2)]
        plan, used = bank_plan()

        adj_t = adjT.rearrange("b (t p) (i n) -> b t p i n", p=P, n=HALF)

        per = {}
        sems = {}

        def sem(name, n=1):
            sems[name] = ctx.enter_context(nc.semaphore(name))
            per[name] = n
            return name

        for part in used:
            for i in range(len(used[part])):
                sem(f"{part}_full{i}", used[part][i])
                sem(f"{part}_free{i}", used[part][i])
        for name, n in (
            ("x_in", 16), ("am_in", 16 * NT), ("am_seen", NT), ("m1_ready", NT), ("an_in", 16 * NT), ("nm_ready", NT),
            ("fl_full", 1), ("fl_read", 1), ("res_ready", 1),
            ("sn_ready", 4), ("lp_ready", 2 * NT), ("lm_ready", 2 * NT), ("e_ready", 2 * NT),
            ("rcp_ready", 2 * NT), ("whs_ready", 2 * NT), ("e_used", 2 * (NT - 1)),
            ("pre_rs", 2), ("post_rs", 2), ("pre_ln", 4), ("post_ln", 4), ("rx_ready", 4),
            ("p1_ready", 2), ("r1_ready", 2), ("p2_ready", 2), ("p3_ready", 2),
            ("stack_in0", 16 * 2 * len(QK_PIECES)), ("stack_in1", 16 * 2 * len(QK_PIECES)),
            ("mx_full", 8 * NT), ("mx_read", 8 * NT),
            ("mneg_ready", 2), ("c1_ready", 2), ("mr_ready", 2), ("c2_ready", 2), ("cm_ready", 2),
            ("ct_full", 2), ("ct_read", 2), ("c_in", 2 * 16 * CROWS),
            ("st_full", 64), ("p_ready", 64), ("pm_ready", 64), ("p_used", 32), ("u_ready", 4),
            ("out_done", 16), ("flag_ready", 1), ("u_done", 2),
            ("r_adj", 16 * STEPS), ("r_xb", STEPS), ("r_v", STEPS), ("r_vc", STEPS), ("r_st", STEPS), ("r_p", STEPS),
            ("r_below", STEPS), ("r_mask", STEPS), ("r_pm", 3 * STEPS), ("r_acc", 3 * STEPS), ("r_done", STEPS),
        ):
            sem(name, n)
        w_in = ctx.enter_context(nc.semaphore("w_in"))
        made = ctx.enter_context(nc.semaphore("made"))
        dmade = ctx.enter_context(nc.semaphore("dmade"))
        flag_seen = ctx.enter_context(nc.semaphore("flag_seen"))
        tile_there = ctx.enter_context(nc.semaphore("tile_there"))
        lp_seen = ctx.enter_context(nc.semaphore("lp_seen"))
        wo_zero = ctx.enter_context(nc.semaphore("wo_zero"))
        pmade = ctx.enter_context(nc.semaphore("pmade"))
        prep_full = ctx.enter_context(nc.semaphore("prep_full"))

        AHEAD = {"r_done"}

        def graph_of(g, shift):
            return g[0], g[1] + shift

        def is_graph(g, number):
            return isinstance(g[0], int) and g[0] + g[1] == number

        def is_first(g):
            return is_graph(g, 0)

        def at(name, b, n):
            return sems[name], b[0] * per[name] + (b[1] * per[name] + n + (name in AHEAD))

        def bank_idle(b, key):
            part, i, n = plan[key]
            return at(f"{part}_free{i}", b, n)

        def first_use(key):
            return plan[key][2] == 0

        def bank_full(b, key):
            part, i, n = plan[key]
            return at(f"{part}_full{i}", b, n + 1)

        def bank_read(b, key):
            part, i, n = plan[key]
            return at(f"{part}_free{i}", b, n + 1)

        def full(key):
            return sems[f"{plan[key][0]}_full{plan[key][1]}"]

        def free(key):
            return sems[f"{plan[key][0]}_free{plan[key][1]}"]

        def bank(key):
            part, i, _ = plan[key]
            return {"gat": ms[0:2], "pre": [ms[2], pv], "val": ms[0:2], "post": ms[0:2]}[part][i]

        def hs(half):
            return slice(half * HALF, (half + 1) * HALF)

        def at_step(name, step, n):
            return sems[name], step * (per[name] // STEPS) + n + (name in AHEAD)

        def v_of(t, w, h):
            first = ((t * 2 + w) * NH + h) * VW
            return VV[:, first:first + 32]

        def step_number(b, g, t, it):
            return (((b[0] + b[1]) * 2 + g) * NT + t) * NHALF + it

        MAX_TICKS = NH * NT
        ATT = 4 * NT
        CT_TICK = MAX_TICKS // 2 + 2
        FLAG_TICK = 54
        M1_TICKS = [5, 10, 15, 21, 26, 34, 39, 44]
        NM_TICKS = [7, 12, 17, 23, 28, 36, 41, 50]

        def first_step(side, n):
            if n % (2 * NT) != NT + 1:
                next(side, None)

        def second_step(side, n):
            if n % (2 * NT) < 2:
                next(side, None)

        NW = 5 + NH
        block = ctx.enter_context(nc.Block())

        VAL, HEAD, LN, FF, GAT, QKV, SPLIT = NT // 2 + 1, 11, 9, 20, 9 + NT, 4, 8

        def idle(steps):
            for _ in range(steps):
                yield

        def both(one, other):
            while True:
                ended = [next(thread, "end") == "end" for thread in (one, other)]
                if all(ended):
                    return
                yield

        def layers_of(parts, b, has_post, has_pre):
            _, pre, val, post = parts

            def last():
                yield from val(b, has_post, has_pre)
                if has_post:
                    yield from post(graph_of(b, -1), True)

            return both(last(), pre(graph_of(b, 1), True) if has_pre else iter(()))

        def gat_of(parts, b, has_gat):
            if has_gat:
                yield from parts[0](graph_of(b, 2))

        def rest(side):
            for _ in side:
                pass

        @block.sync
        def _(sp):
            sp.dma_start(MAT[:, :], mats).then_inc(w_in, 16)
            sp.dma_start(GWT, gwt.rearrange("(k p) f -> p k f", k=2)).then_inc(w_in, 16)
            sp.dma_start(COL[:, :], cols).then_inc(w_in, 16)
            sp.dma_start(WVR, wv).then_inc(w_in, 16)
            sp.dma_start(BV, bv.rearrange("(o r) f -> o r f", o=1).to_broadcast([P, 4, P])).then_inc(w_in, 16)
            sp.wait_ge(wo_zero, 1)
            for h in range(NH):
                sp.dma_start(WO[32 * (h % 4):32 * (h % 4) + DH, h // 4, :], wo[h * DH:(h + 1) * DH, :]).then_inc(w_in, 16)

            def load_x(b, first):
                if not first:
                    sp.wait_ge(*bank_read(graph_of(b, -1), ("gout", 1, 1)))
                sp.dma_start(XT[:, :], xT[b[0] + b[1]]).then_inc(sems["x_in"], 16)

            def load_am(b, t, first):
                if t > 0 or not first:
                    sp.wait_ge(*at("m1_ready", b, t))
                    sp.wait_ge(*at("am_seen", b, t))
                sp.dma_start(AM[:, :], adjT[b[0] + b[1], t * P:(t + 1) * P, :]).then_inc(sems["am_in"], 16)

            def load_an(b, t):
                if t > 0 or not is_first(b):
                    sp.wait_ge(*at("nm_ready", b, t))
                sp.dma_start(AN[:, :], adjT[b[0] + b[1], t * P:(t + 1) * P, :]).then_inc(sems["an_in"], 16)

            def stack(b, g):
                for piece, ready in ((0, "p1_ready"), (1, "p2_ready"), (2, "p3_ready")):
                    for w, dst in enumerate((QS, KS)):
                        sp.wait_ge(*at(ready, b, w + 1))
                        for slot, pair in enumerate(QK_PIECES):
                            if pair[w] == piece:
                                sp.dma_start(dst[slot * DH:(slot + 1) * DH, 4 * g:4 * g + 4, :],
                                             QP[64 * g:64 * g + 64, w, piece, :]).then_inc(sems[f"stack_in{g}"], 16)

            def negated_maxima(b, g):
                sp.wait_ge(*at("ct_read", b, g + 1))
                for c in range(CROWS):
                    sp.dma_start(QS[KROWS + c:KROWS + c + 1, 4 * g:4 * g + 4, :],
                                 CR[4 * c:4 * c + 4, :]).then_inc(sems["c_in"], 16)

            def val(b, has_post, has_pre):
                yield from idle(VAL)

            def post(b, in_loop):
                yield from idle(HEAD + 2 * LN + FF)
                sp.wait_ge(*at("post_ln", b, 4))
                sp.dma_start(outT[b[0] + b[1]], OT).then_inc(sems["out_done"], 16)

            def pre(b, has_post):
                yield from idle(2 * LN + FF + QKV + SPLIT)

            def gat(b):
                yield from idle(2 * GAT)

            def main(b, has_post, has_pre, has_gat):
                load_am(b, 0, not has_post)
                if has_gat:
                    load_x(graph_of(b, 2), False)
                    load_an(graph_of(b, 2), 0)
                if has_post:
                    sp.wait_ge(*at("u_done", b, 0))
                stack(b, 1)
                side = layers_of((gat, pre, val, post), b, has_post, has_pre)
                for tick in range(MAX_TICKS):
                    if tick - 2 in M1_TICKS[:-1]:
                        load_am(b, M1_TICKS.index(tick - 2) + 1, False)
                    if has_gat and tick - 3 in NM_TICKS[:-1]:
                        load_an(graph_of(b, 2), NM_TICKS.index(tick - 3) + 1)
                    if tick == CT_TICK + 2:
                        negated_maxima(b, 0)
                    next(side, None)
                rest(side)
                negated_maxima(b, 1)
                if has_pre:
                    sp.wait_ge(*at("u_done", b, 1))
                    stack(graph_of(b, 1), 0)

            for g in range(2):
                load_x((0, g), g == 0)
                for t in range(NT):
                    load_an((0, g), t)
            stack((0, 0), 0)
            main((0, 0), False, True, True)
            with sp.Fori(0, B - 3) as c:
                main((c, 1), True, True, True)
            main((0, B - 2), True, True, False)
            main((0, B - 1), True, False, False)
            rest(post((0, B - 1), False))
            sp.wait_ge(*at("out_done", (0, B), 0))

        @block.gpsimd
        def _(pool):
            nc.gpsimd.memset(ZERO, 0.0).then_inc(pmade, 1)
            nc.gpsimd.memset(POW[:, :], -0.5).then_inc(pmade, 1)
            nc.gpsimd.memset(IDF[:, :], 0.0).then_inc(pmade, 1)
            nc.gpsimd.memset(MEAN[:, :], 1.0 / F).then_inc(pmade, 1)
            nc.gpsimd.memset(CEN[:, :], -1.0 / F).then_inc(pmade, 1)
            nc.gpsimd.memset(IDB[:, :], 0.0).then_inc(pmade, 1)
            nc.gpsimd.memset(SEL[:, :], 0.0).then_inc(pmade, 1)
            pool.wait_ge(pmade, 7)
            nc.gpsimd.affine_select(out=CEN[:, :], in_=CEN[:, :], compare_op=ALU.not_equal, fill=1.0 - 1.0 / F,
                                    base=0, pattern=[[-1, P]], channel_multiplier=1).then_inc(pmade, 1)
            nc.gpsimd.affine_select(out=IDB[:, :], in_=IDB[:, :], compare_op=ALU.not_equal, fill=1.0,
                                    base=0, pattern=[[-1, P]], channel_multiplier=1).then_inc(pmade, 1)
            nc.gpsimd.affine_select(out=IDF[:, :], in_=IDF[:, :], compare_op=ALU.not_equal, fill=1.0,
                                    base=0, pattern=[[-1, P]], channel_multiplier=1).then_inc(pmade, 1)
            nc.gpsimd.affine_select(out=SEL[:, :], in_=SEL[:, :], compare_op=ALU.not_equal, fill=1.0, base=-DH,
                                    pattern=[[-32, 4]], channel_multiplier=1).then_inc(pmade, 1)

            def ln(b, i, part):
                yield from idle(4)
                pool.wait_ge(*bank_read(b, ("var", i)))
                FA, SQ, XC, YT, HT, VE, RS = AREAS[part]
                nc.gpsimd.tensor_tensor(RS, VE, POW[:, :], ALU.pow).then_inc(sems[part + "_rs"], 1)
                yield from idle(LN - 4)

            def val(b, has_post, has_pre):
                yield from idle(VAL)

            def post(b, in_loop):
                yield from idle(HEAD)
                yield from ln(b, 2, "post")
                yield from idle(FF)
                yield from ln(b, 3, "post")

            def pre(b, has_post):
                yield from ln(b, 0, "pre")
                yield from idle(FF)
                yield from ln(b, 1, "pre")
                yield from idle(QKV + SPLIT)

            def gat(b):
                yield from idle(2 * GAT)

            def make_m1(b, t, has_post):
                if t == 0 and has_post:
                    pool.wait_ge(*at("u_done", b, 0))
                pool.wait_ge(*at("am_in", b, 16 * (t + 1)))
                pool.sem_inc(tile_there, 1)
                nc.gpsimd.tensor_scalar(M1[:, t, :], AM[:, :], 1.0, None, ALU.is_equal).then_inc(sems["m1_ready"], 1)

            def make_nm(b, t):
                if t == 0:
                    pool.wait_ge(*at("lm_ready", b, 0))
                pool.wait_ge(*at("an_in", b, 16 * (t + 1)))
                pool.sem_inc(tile_there, 1)
                nc.gpsimd.tensor_scalar(NM[:, t, :], AN[:, :], 0.0, FAR, ALU.is_le, ALU.mult).then_inc(sems["nm_ready"], 1)

            def main(b, has_post, has_pre, has_gat):
                side = layers_of((gat, pre, val, post), b, has_post, has_pre)
                for tick in range(MAX_TICKS):
                    if tick in M1_TICKS:
                        make_m1(b, M1_TICKS.index(tick), has_post)
                    if has_gat and tick in NM_TICKS:
                        make_nm(graph_of(b, 2), NM_TICKS.index(tick))
                    next(side, None)
                rest(side)

            rest(pre((0, 0), False))
            main((0, 0), False, True, True)
            with pool.Fori(0, B - 3) as c:
                main((c, 1), True, True, True)
            main((0, B - 2), True, True, False)
            main((0, B - 1), True, False, False)
            rest(post((0, B - 1), False))

        @block.scalar
        def _(act):
            act.sem_inc(sems["r_done"], 1)
            act.wait_ge(w_in, 16 * NW)
            act.wait_ge(dmade, 15)
            nc.scalar.mul(BQ4[:, :], col("bq"), 0.25).then_inc(made, 1)
            act.wait_ge(made, 1)
            for k, name in enumerate(("a1s", "a2s")):
                act.wait_ge(pmade, 11)
                nc.scalar.activation(AREP[:, k, :], ZERO, ACT.Identity, bias=col(name)).then_inc(made, 1)
            for k in range(2):
                act.wait_ge(prep_full, k + 1)
                nc.scalar.mul(WREP[:, k, :], st[k][:, 0, 0:P], -1.0).then_inc(made, 1)
                nc.scalar.mul(WX[:, k, P:P + 1], st[k][:, 1, 0:1], -0.8).then_inc(made, 1)
                nc.scalar.copy(WX[:, k, 0:P], gW[k]).then_inc(made, 1)

            def ln(b, i, part, be, dst=None):
                FA, SQ, XC, YT, HT, VE, RS = AREAS[part]
                dst = HT if dst is None else dst
                yield
                for half in range(2):
                    key = ("xc", i, half)
                    act.wait_ge(*bank_full(b, key))
                    nc.scalar.copy(XC[:, half, :], bank(key)[:, :])
                    nc.scalar.activation(SQ[:, half, :], bank(key)[:, :], ACT.Square).then_inc(free(key), 1)
                    yield
                yield from idle(LN - 4)
                for half in range(2):
                    act.wait_ge(*bank_read(b, ("bc", i, half)))
                    if i == 1 and half == 0 and not is_first(b):
                        act.wait_ge(*at("res_ready", b, 0))
                    nc.scalar.activation(dst[:, hs(half)], XC[:, half, :], ACT.Identity, bias=col(be)).then_inc(
                        sems[part + "_ln"], 1)
                yield

            def ff(b, i, part, func, bias):
                FA = AREAS[part][0]
                for half in range(2):
                    yield
                    for c in range(HC):
                        key = ("f1", i, half, c)
                        act.wait_ge(*bank_full(b, key))
                        nc.scalar.activation(FA[:, c, :], bank(key)[:, :], func, bias=col(bias, c)).then_inc(free(key), 1)
                        yield from idle(2)
                    yield

            def keep_input(b, before):
                if before is not None:
                    act.wait_ge(*bank_read(before, ("wo", 1)))
                act.wait_ge(*at("pre_ln", b, 4))
                nc.scalar.copy(RES[:, :], X2[:, :]).then_inc(sems["res_ready"], 1)

            def val(b, has_post, has_pre):
                if not has_post:
                    keep_input(b, None)
                yield from idle(VAL)

            def post(b, in_loop):
                yield from idle(2)
                act.wait_ge(*bank_read(b, ("sm",)))
                act.wait_ge(*at("u_done", b, 2))
                FA = AREAS["post"][0]
                for gi in range(4):
                    nc.scalar.copy(FA[:, gi, :].rearrange("p (a k) -> p a k", k=32),
                                   RCP[:, 4 * gi:4 * gi + 4, :].rearrange("p a (h o) -> p (a h) o", o=1)
                                   .to_broadcast([P, 16, 32])).then_inc(sems["rx_ready"], 1)
                    yield
                yield from idle(HEAD - 6)
                if in_loop:
                    keep_input(graph_of(b, 1), b)
                yield from ln(b, 2, "post", "be1")
                yield from ff(b, 1, "post", ACT.Gelu, "b1")
                yield from ln(b, 3, "post", "be2", OT)

            def seen(b, t, has_post):
                act.wait_ge(*at("am_in", b, 16 * (t + 1)))
                if t == 0 and has_post:
                    act.wait_ge(*at("u_done", b, 0))
                if t >= 1 or has_post:
                    act.wait_ge(*at("am_seen", b, t))
                nc.scalar.activation(SEEN, AM[:, :], ACT.Square, bias=HALFN[:, :],
                                     accum_out=CHK[:, t:t + 1]).then_inc(sems["am_seen"], 1)

            def gat(b):
                for k in range(2):
                    yield
                    for half in range(2):
                        key = ("s", k, half)
                        act.wait_ge(*bank_full(b, key))
                        nc.scalar.mul(SN2[:, hs(half)], bank(key)[:, :], 0.2).then_inc(sems["sn_ready"], 1)
                        nc.scalar.copy(SN[:, hs(half)], bank(key)[:, :]).then_inc(free(key), 1)
                        yield
                    for w in range(3):
                        key = ("wh", k, w)
                        act.wait_ge(*bank_full(b, key))
                        n = min(3, NT - 3 * w)
                        nc.scalar.copy(WH[:, 3 * w:3 * w + n, :],
                                       bank(key)[:, 0:n * (P + 1)].rearrange("p (t f) -> p t f", t=n)).then_inc(free(key), 1)
                        if w < 2:
                            yield
                    for j in range(NT + 3):
                        t = j - 1
                        if 0 <= t < NT:
                            act.wait_ge(*at("lm_ready", b, NT * k + t + 1))
                            e = LP[t % 5][:, :, :].rearrange("p a n -> p (a n)")
                            nc.scalar.activation(e, e, ACT.Exp, scale=-1.0, bias=LMIN[:, t:t + 1],
                                                 accum_out=ESUM[:, t:t + 1]).then_inc(sems["e_ready"], 1)
                        yield
                    if k == 0:
                        for half in range(2):
                            key = ("gout", 0, half)
                            act.wait_ge(*bank_full(b, key))
                            nc.scalar.copy(H1[:, hs(half)], bank(key)[:, :]).then_inc(free(key), 1)
                    yield

            def pre(b, has_post):
                if not is_graph(b, 0) and not is_graph(b, 1):
                    act.wait_ge(*at("u_done", graph_of(b, -1), 0))
                yield from ln(b, 0, "pre", "bln1")
                yield from ff(b, 0, "pre", ACT.Relu, "bff1")
                yield from ln(b, 1, "pre", "bln2", X2)
                for w, half in ((0, 0), (0, 1), (1, 0), (1, 1)):
                    if half == 0:
                        yield
                    key = ("qk"[w], half)
                    act.wait_ge(*bank_full(b, key))
                    nc.scalar.activation(QK[:, w, hs(half)], bank(key)[:, :], ACT.Identity,
                                         bias=BQ4[:, :] if w == 0 else col("bk"),
                                         scale=0.25 if w == 0 else 1.0).then_inc(free(key), 1)
                    if half == 1:
                        yield
                for w in range(2):
                    for half in range(2):
                        act.wait_ge(*bank_read(b, ("qk"[w], half)))
                    if w == 0 and not is_first(b):
                        act.wait_ge(*at("stack_in0", b, 0))
                        act.wait_ge(*at("stack_in1", b, 0))
                    nc.scalar.copy(QP[:, w, 0, :], QK[:, w, :]).then_inc(sems["p1_ready"], 1)
                    yield
                yield from idle(2)
                for w in range(2):
                    act.wait_ge(*at("r1_ready", b, w + 1))
                    nc.scalar.copy(QP[:, w, 1, :], QK[:, w, :]).then_inc(sems["p2_ready"], 1)
                    yield
                yield from idle(2)

            def maxima_out(b, g):
                act.wait_ge(*at("ct_full", b, g + 1))
                if g == 1:
                    act.wait_ge(*at("c_in", b, 16 * CROWS))
                elif not is_first(b):
                    act.wait_ge(*at("c_in", b, 0))
                ct = (st[(CT_TICK + 1) % 2][:, 0, :], pv[:, :])[g]
                nc.scalar.copy(CR[:, :], ct.bitcast(BF16)[0:CROWS * 4, :]).then_inc(sems["ct_read"], 1)

            def output_out(b, n, has_post):
                act.wait_ge(*at("p_used", b, n))
                gi = n // NT - 1
                if gi == 0 and has_post:
                    act.wait_ge(*bank_full(graph_of(b, -1), ("wo", 1)))
                nc.scalar.copy(U[:, gi, :], pv[:, :]).then_inc(sems["u_ready"], 1)

            def general_step(b, t, it, g, step):
                act.wait_ge(*at_step("r_done", step, 0))
                act.dma_start(AR, adj_t[b[0] + b[1], t, :, it, :]).then_inc(sems["r_adj"], 16)
                nc.scalar.copy(XB, RES[:, :].rearrange("p (t n) -> p t n", t=NT)[:, t, :]).then_inc(sems["r_xb"], 1)
                act.wait_ge(*at_step("r_st", step, 1))
                for pr in range(2):
                    ins = nc.scalar.activation(PT[:, 0, 2 * pr:2 * pr + 2, :], st[pr][:, :, :], ACT.Exp)
                ins.then_inc(sems["r_p"], 1)

            def main(b, has_post, has_pre, has_gat):
                side = layers_of((gat, pre, val, post), b, has_post, has_pre)
                for tick in range(MAX_TICKS):
                    if tick in M1_TICKS:
                        seen(b, M1_TICKS.index(tick), has_post)
                    if tick == CT_TICK:
                        maxima_out(b, 0)
                    next(side, None)
                rest(side)
                act.wait_ge(*at("am_seen", b, NT))
                if has_pre:
                    act.wait_ge(*at("p3_ready", graph_of(b, 1), 2))
                side = gat_of((gat, pre, val, post), b, has_gat)
                for n in range(ATT):
                    g = n // (2 * NT)
                    if n % (2 * NT) == 0 and (g == 1 or not is_first(b)):
                        act.wait_ge(*at("u_done", b, g))
                    for pr in range(2):
                        act.wait_ge(*at("st_full", b, 2 * n + pr + 1))
                        if pr == 0 and n % (2 * NT) >= 3:
                            act.wait_ge(*at("p_used", b, n - 2))
                        nc.scalar.activation(PT[:, n % 3, 2 * pr:2 * pr + 2, :], st[pr][:, :, :], ACT.Exp).then_inc(
                            sems["p_ready"], 1)
                    if n == 0:
                        maxima_out(b, 1)
                    first_step(side, n)
                    if n % (2 * NT) == NT:
                        output_out(b, n, has_post)
                    if n % (2 * NT) == 2 * NT - 1:
                        output_out(b, n + 1, has_post)
                        act.wait_ge(*at("flag_ready", b, 1))
                        act.sem_inc(flag_seen, 1)
                        flag = act.value_load(FLAG[0:1, 0:1], min_val=0, max_val=1)
                        with act.If(flag == 1):
                            with act.Fori(0, NT) as t:
                                with act.Fori(0, NHALF) as it:
                                    general_step(b, t, it, g, step_number(b, g, t, it))
                        with act.Else():
                            for name in ("r_adj", "r_xb", "r_p"):
                                act.sem_inc(sems[name], per[name] // 2)
                    second_step(side, n)
                rest(side)

            rest(gat((0, 0)))
            rest(both(pre((0, 0), False), gat((0, 1))))
            main((0, 0), False, True, True)
            with act.Fori(0, B - 3) as c:
                main((c, 1), True, True, True)
            main((0, B - 2), True, True, False)
            main((0, B - 1), True, False, False)
            rest(post((0, B - 1), False))

        @block.vector
        def _(dve):
            nc.vector.memset(WO[:, :, :], 0.0).then_inc(wo_zero, 1)
            nc.vector.memset(VV[:, :], 0.0).then_inc(dmade, 1)
            nc.vector.memset(KS[KROWS:P, :, :], 1.0).then_inc(dmade, 1)
            nc.vector.memset(VC[:, :, :, :], 0.0).then_inc(dmade, 1)
            nc.vector.memset(HALFN[:, :], -0.5).then_inc(dmade, 1)
            dve.wait_ge(dmade, 4)
            nc.vector.memset(V4[:, :, 0, :, DH:DH + 1], 1.0).then_inc(dmade, 1)
            dve.wait_ge(w_in, 16 * NW)
            nc.vector.tensor_copy(WV[:, 0, :], WVR[:, 0, :]).then_inc(dmade, 1)
            nc.vector.tensor_copy(BVD[:, 0, :], BV[:, 0, :]).then_inc(dmade, 1)
            nc.vector.tensor_tensor(WV[:, 1, :], WVR[:, 1, :], WVR[:, 0, :], ALU.subtract).then_inc(dmade, 1)
            nc.vector.tensor_tensor(BVD[:, 1, :], BV[:, 1, :], BV[:, 0, :], ALU.subtract).then_inc(dmade, 1)
            for dst, src in ((WVX, WVR), (BVX, BV)):
                for r in range(2):
                    nc.vector.tensor_tensor(dst[:, r, :], src[:, 2 + r, :], src[:, 0, :], ALU.subtract).then_inc(dmade, 1)
                nc.vector.tensor_scalar(dst[:, 2, :], src[:, 0, :], -1.0, None, ALU.mult).then_inc(dmade, 1)

            def ln(b, i, part, g):
                FA, SQ, XC, YT, HT, VE, RS = AREAS[part]
                yield from idle(4)
                key = ("var", i)
                dve.wait_ge(*bank_full(b, key))
                nc.vector.tensor_scalar(VE, bank(key)[:, 0:NT], EPS, None, ALU.add).then_inc(free(key), 1)
                yield from idle(2)
                for half in range(2):
                    key = ("bc", i, half)
                    dve.wait_ge(*bank_full(b, key))
                    nc.vector.scalar_tensor_tensor(out=XC[:, half, :], in0=XC[:, half, :], scalar=col(g),
                                                   in1=bank(key)[:, :], op0=ALU.mult, op1=ALU.mult).then_inc(free(key), 1)
                    yield
                yield

            def ff_out(b, i, part, bias):
                FA, SQ, XC, YT, HT, VE, RS = AREAS[part]
                for half in range(2):
                    yield from idle(FF // 2 - 1)
                    key = ("f2", i, half)
                    dve.wait_ge(*bank_full(b, key))
                    nc.vector.scalar_tensor_tensor(out=YT[:, hs(half)], in0=bank(key)[:, :], scalar=col(bias),
                                                   in1=HT[:, hs(half)], op0=ALU.add, op1=ALU.add).then_inc(free(key), 1)
                    yield

            def val(b, has_post, has_pre):
                if has_post:
                    dve.wait_ge(*at("p_used", b, 0))
                else:
                    dve.wait_ge(dmade, 15)
                yield
                for i in range(NT // 2):
                    key = ("v", i)
                    dve.wait_ge(*bank_full(b, key))
                    for j in range(2):
                        ins = nc.vector.tensor_tensor(
                            V4[:, 2 * i + j, :, :, 0:DH].rearrange("p w h d -> p (w h) d"),
                            bank(key)[:, 256 * j:256 * (j + 1)].rearrange("p (g d) -> p g d", d=DH),
                            BVD[:, :, :].rearrange("p w (h d) -> p (w h) d", d=DH), ALU.add)
                    ins.then_inc(free(key), 1)
                    yield

            def post(b, in_loop):
                yield
                key = ("sm",)
                dve.wait_ge(*bank_full(b, key))
                nc.vector.reciprocal(RCP[:, :, :].rearrange("p a h -> p (a h)"), bank(key)[:, 0:64]).then_inc(free(key), 1)
                yield from idle(3)
                for gi in range(4):
                    key = ("rb", gi)
                    dve.wait_ge(*bank_full(b, key))
                    nc.vector.tensor_tensor(U[:, gi, :], U[:, gi, :], bank(key)[:, :], ALU.mult).then_inc(free(key), 1)
                    yield
                yield
                for half in range(2):
                    key = ("wo", half)
                    dve.wait_ge(*bank_full(b, key))
                    if half == 0:
                        dve.wait_ge(*at("res_ready", b, 1))
                        if not in_loop:
                            dve.wait_ge(*at("out_done", b, 0))
                    nc.vector.scalar_tensor_tensor(out=OT[:, hs(half)], in0=bank(key)[:, :], scalar=col("bo"),
                                                   in1=RES[:, hs(half)], op0=ALU.add, op1=ALU.add).then_inc(free(key), 1)
                    yield
                yield from ln(b, 2, "post", "g1")
                yield from ff_out(b, 1, "post", "b2")
                yield from ln(b, 3, "post", "g2")

            def make_nm(b, t):
                dve.wait_ge(*at("an_in", b, 16 * (t + 1)))
                nc.vector.tensor_scalar(NM[:, t, :], AN[:, :], 0.0, FAR, ALU.is_le, ALU.mult).then_inc(sems["nm_ready"], 1)

            def logits(b, k, t):
                if t == 0:
                    for half in range(2):
                        dve.wait_ge(*bank_read(b, ("s", k, half)))
                if t % 3 == 0:
                    dve.wait_ge(*bank_read(b, ("wh", k, t // 3)))
                if t >= 5:
                    dve.wait_ge(*at("e_used", b, (NT - 1) * k + t - 4))
                nc.vector.scalar_tensor_tensor(out=LP[t % 5][:, :, :].rearrange("p a n -> p (a n)"), in0=SN[:, :],
                                               scalar=WH[:, t, P:P + 1], in1=SN2[:, :], op0=ALU.add, op1=ALU.min).then_inc(sems["lp_ready"], 1)

            def masked(b, k, t):
                if k == 0:
                    dve.wait_ge(*at("nm_ready", b, t + 1))
                dve.wait_ge(*at("lp_ready", b, NT * k + t + 1))
                dve.sem_inc(lp_seen, 1)
                lp = LP[t % 5][:, :, :].rearrange("p a n -> p (a n)")
                nc.vector.tensor_tensor_reduce(out=lp, in0=lp, in1=NM[:, t, :],
                                               scale=1.0, scalar=3e38, op0=ALU.add, op1=ALU.min,
                                               accum_out=LMIN[:, t:t + 1]).then_inc(sems["lm_ready"], 1)

            def norm(b, k, t):
                dve.wait_ge(*at("e_ready", b, NT * k + t + 1))
                nc.vector.reciprocal(ERCP[:, t:t + 1], ESUM[:, t:t + 1]).then_inc(sems["rcp_ready"], 1)
                dve.wait_ge(*at("rcp_ready", b, NT * k + t + 1))
                if t >= 4:
                    dve.wait_ge(*at("e_used", b, (NT - 1) * k + t - 3))
                nc.vector.tensor_scalar(WHS[:, t % 4, :], WH[:, t, 0:P], ERCP[:, t:t + 1], None, ALU.mult).then_inc(
                    sems["whs_ready"], 1)

            def gat(b):
                here = isinstance(b[0], int) and b[0] + b[1] < 2
                for k in range(2):
                    yield from idle(4)
                    if k == 0 and here:
                        if not is_first(b):
                            dve.wait_ge(*at("lm_ready", b, 0))
                        make_nm(b, 0)
                    yield
                    logits(b, k, 0)
                    for j in range(NT + 3):
                        if k == 0 and here and j + 1 < NT:
                            make_nm(b, j + 1)
                        if j + 1 < NT:
                            logits(b, k, j + 1)
                        if j < NT:
                            masked(b, k, j)
                        if 0 <= j - 2 < NT:
                            norm(b, k, j - 2)
                        yield
                    if k == 1:
                        for half in range(2):
                            key = ("gout", 1, half)
                            dve.wait_ge(*bank_full(b, key))
                            if half == 0:
                                dve.wait_ge(*at("x_in", b, 16))
                            nc.vector.tensor_tensor(H1[:, hs(half)], bank(key)[:, :], XT[:, hs(half)], ALU.add).then_inc(free(key), 1)
                    yield

            def pre(b, has_post):
                yield from ln(b, 0, "pre", "gln1")
                yield from ff_out(b, 0, "pre", "bff2")
                yield from ln(b, 1, "pre", "gln2")
                yield from idle(QKV)
                for piece, rounded in ((0, "p1_ready"), (1, "p2_ready")):
                    yield from idle(2)
                    for w in range(2):
                        dve.wait_ge(*at(rounded, b, w + 1))
                        if piece == 0:
                            nc.vector.tensor_tensor(QK[:, w, :], QK[:, w, :], QP[:, w, 0, :], ALU.subtract).then_inc(
                                sems["r1_ready"], 1)
                        else:
                            nc.vector.tensor_tensor(QP[:, w, 2, :], QK[:, w, :], QP[:, w, 1, :], ALU.subtract).then_inc(
                                sems["p3_ready"], 1)
                        yield

            def pieces_of_maxima(b, g):
                dve.wait_ge(*at("mx_read", b, 4 * NT * (g + 1)))
                nc.vector.tensor_scalar(MNEG[:, g], MX[:, g], -1.0, None, ALU.mult).then_inc(sems["mneg_ready"], 1)
                dve.wait_ge(*at("mneg_ready", b, g + 1))
                nc.vector.tensor_copy(CM[:, g, :, 0, :], MNEG[:, g]).then_inc(sems["c1_ready"], 1)
                dve.wait_ge(*at("c1_ready", b, g + 1))
                nc.vector.tensor_tensor(MR[:, g], MNEG[:, g], CM[:, g, :, 0, :], ALU.subtract).then_inc(sems["mr_ready"], 1)
                dve.wait_ge(*at("mr_ready", b, g + 1))
                nc.vector.tensor_copy(CM[:, g, :, 1, :], MR[:, g]).then_inc(sems["c2_ready"], 1)
                dve.wait_ge(*at("c2_ready", b, g + 1))
                nc.vector.tensor_tensor(CM[:, g, :, 2, :], MR[:, g], CM[:, g, :, 1, :], ALU.subtract).then_inc(sems["cm_ready"], 1)

            def general_step(t, it, g, step):
                dve.wait_ge(*at_step("r_done", step, 0))
                dve.wait_ge(*at_step("r_v", step, 1))
                vx = pv[:, 0:3 * P].rearrange("p (r g f) -> p r g f", r=3, g=2)
                bx = BVX[:, :, :].rearrange("p r (g f) -> p r g f", g=2)
                for r in range(3):
                    ins = nc.vector.tensor_tensor(VC[:, r, :, 0:DH], vx[:, r, g, :].rearrange("p (h d) -> p h d", d=DH),
                                                  bx[:, r, g, :].rearrange("p (h d) -> p h d", d=DH), ALU.add)
                ins.then_inc(sems["r_vc"], 1)
                dve.wait_ge(*at_step("r_adj", step, 16))
                nc.vector.tensor_scalar(BELOW, AR, 0.0, None, ALU.is_lt).then_inc(sems["r_below"], 1)
                nc.vector.tensor_scalar(MK[:, 0, :], AR, 2.0, None, ALU.is_equal)
                nc.vector.tensor_scalar(MK[:, 1, :], AR, 3.0, None, ALU.is_equal)
                dve.wait_ge(*at_step("r_below", step, 1))
                nc.vector.scalar_tensor_tensor(out=MK[:, 2, :], in0=AR, scalar=3.0, in1=BELOW,
                                               op0=ALU.is_gt, op1=ALU.add).then_inc(sems["r_mask"], 1)
                dve.wait_ge(*at_step("r_mask", step, 1))
                dve.wait_ge(*at_step("r_p", step, 1))
                for r in range(3):
                    if r == 2:
                        dve.wait_ge(*at_step("r_acc", step, 1))
                    nc.vector.tensor_tensor(PM[:, r % 2, :, :], PT[:, 0, :, :],
                                            MK[:, r:r + 1, :].to_broadcast([P, 4, HALF]), ALU.mult).then_inc(sems["r_pm"], 1)
                dve.wait_ge(*at_step("r_acc", step, 3))
                u = U[:, :, :].rearrange("p (g i) n -> p g i n", g=2)[:, g, it, :]
                nc.vector.tensor_tensor(u, u, pv[:, :], ALU.add).then_inc(sems["r_done"], 1)

            def general_flag(b):
                dve.wait_ge(*at("fl_full", b, 1))
                nc.vector.reduce_max(FMAX[:, :], st[(FLAG_TICK + 1) % 2][:, 0, 0:NT], AX.X).then_inc(sems["fl_read"], 1)
                dve.wait_ge(*at("fl_read", b, 1))
                nc.vector.tensor_scalar(FLAG[:, :], FMAX[:, :], N / 4.0, None, ALU.is_gt).then_inc(sems["flag_ready"], 1)

            def main(b, has_post, has_pre, has_gat):
                side = layers_of((gat, pre, val, post), b, has_post, has_pre)
                for tick in range(MAX_TICKS):
                    g, h, t = tick // (4 * NT), tick // NT % 4, tick % NT
                    dve.wait_ge(*at("mx_full", b, tick + 1))
                    nc.vector.reduce_max(MX[:, g, t, h:h + 1], st[tick % 2][:, :, :].rearrange("p a n -> p (a n)"),
                                         AX.X).then_inc(sems["mx_read"], 1)
                    if tick % (4 * NT) == 4 * NT - 1:
                        pieces_of_maxima(b, g)
                    if tick == FLAG_TICK:
                        if has_post:
                            dve.wait_ge(*at("r_acc", b, 0))
                            dve.wait_ge(*at("r_p", b, 0))
                        general_flag(b)
                    next(side, None)
                rest(side)
                if has_post:
                    dve.wait_ge(*at("out_done", graph_of(b, -1), 16))
                if has_pre:
                    dve.wait_ge(*at("p3_ready", graph_of(b, 1), 2))
                dve.wait_ge(*at("m1_ready", b, NT))
                side = gat_of((gat, pre, val, post), b, has_gat)
                for n in range(ATT):
                    g, it, t = n // (NHALF * NT), n // NT % NHALF, n % NT
                    for pr in range(2):
                        dve.wait_ge(*at("p_ready", b, 2 * n + pr + 1))
                        if pr == 0 and n % (2 * NT) >= 2:
                            dve.wait_ge(*at("p_used", b, n - 1))
                        nc.vector.tensor_tensor(
                            PM[:, n % 2, 2 * pr:2 * pr + 2, :], PT[:, n % 3, 2 * pr:2 * pr + 2, :],
                            M1[:, t:t + 1, hs(it)].to_broadcast([P, 2, HALF]), ALU.mult).then_inc(sems["pm_ready"], 1)
                    first_step(side, n)
                    if n % (2 * NT) == 2 * NT - 1:
                        dve.wait_ge(*at("u_ready", b, 2 * g + 2))
                        dve.wait_ge(*at("flag_ready", b, 1))
                        dve.sem_inc(flag_seen, 1)
                        flag = dve.value_load(FLAG[0:1, 0:1], min_val=0, max_val=1)
                        with dve.If(flag == 1):
                            with dve.Fori(0, NT) as tt:
                                with dve.Fori(0, NHALF) as ii:
                                    general_step(tt, ii, g, step_number(b, g, tt, ii))
                        with dve.Else():
                            for name in ("r_vc", "r_below", "r_mask", "r_pm", "r_done"):
                                dve.sem_inc(sems[name], per[name] // 2)
                        dve.wait_ge(*at("r_done", b, STEPS // 2 * (g + 1)))
                        dve.sem_inc(sems["u_done"], 1)
                    second_step(side, n)
                rest(side)

            rest(gat((0, 0)))
            rest(both(pre((0, 0), False), gat((0, 1))))
            main((0, 0), False, True, True)
            with dve.Fori(0, B - 3) as c:
                main((c, 1), True, True, True)
            main((0, B - 2), True, True, False)
            main((0, B - 1), True, False, False)
            rest(post((0, B - 1), False))

        @block.tensor
        def _(pe):
            pe.wait_ge(w_in, 16 * NW)
            pe.wait_ge(pmade, 11)
            pe.wait_ge(dmade, 15)
            for k in range(2):
                pe.wait_ge(made, 3)
                nc.tensor.matmul(st[k][:, 0, 0:P], GWT[:, k, :], AREP[:, k, :], start=True, stop=True)
                nc.tensor.matmul(st[k][:, 1, 0:1], GWT[:, k, :], col(("a1t", "a2t")[k]), start=True, stop=True).then_inc(prep_full, 1)
            pe.wait_ge(made, 9)

            def part_begins(b, part):
                for i in range(len(used[part])):
                    pe.wait_ge(*at(f"{part}_free{i}", b, used[part][i]))

            def ln(b, i, part, made_by, src=None):
                FA, SQ, XC, YT, HT, VE, RS = AREAS[part]
                src = YT if src is None else src
                for half in range(2):
                    key = ("xc", i, half)
                    pe.wait_ge(*bank_read(b, made_by(half)))
                    if not first_use(key):
                        pe.wait_ge(*bank_idle(b, key))
                    nc.tensor.matmul(bank(key)[:, :], CEN[:, :], src[:, hs(half)], start=True, stop=True).then_inc(full(key), 1)
                    yield
                yield
                pe.wait_ge(*bank_read(b, ("xc", i, 0)))
                pe.wait_ge(*bank_read(b, ("xc", i, 1)))
                key = ("var", i)
                pe.wait_ge(*bank_idle(b, key))
                for t in range(NT):
                    ins = nc.tensor.matmul(bank(key)[:, t:t + 1], SQ[:, t // 4, t % 4 * P:(t % 4 + 1) * P], MEAN[:, 0:1],
                                           start=True, stop=True)
                ins.then_inc(full(key), 1)
                yield from idle(2)
                pe.wait_ge(*at(part + "_rs", b, i % 2 + 1))
                for half in range(2):
                    key = ("bc", i, half)
                    pe.wait_ge(*bank_idle(b, key))
                    for c in range(4):
                        t = 4 * half + c
                        ins = nc.tensor.transpose(bank(key)[:, c * P:(c + 1) * P], RS[:, t:t + 1].to_broadcast([P, P]),
                                                  IDF[:, :])
                    ins.then_inc(full(key), 1)
                    yield
                yield from idle(2)

            def ff(b, i, part, w1, w2):
                FA, SQ, XC, YT, HT, VE, RS = AREAS[part]

                def up(half, c):
                    key = ("f1", i, half, c)
                    pe.wait_ge(*bank_idle(b, key))
                    nc.tensor.matmul(bank(key)[:, :], w1[:, c * P:(c + 1) * P], HT[:, hs(half)],
                                     start=True, stop=True).then_inc(full(key), 1)

                def down(half, c):
                    key = ("f2", i, half)
                    pe.wait_ge(*bank_read(b, ("f1", i, half, c)))
                    if c == 0:
                        pe.wait_ge(*bank_idle(b, key))
                    ins = nc.tensor.matmul(bank(key)[:, :], w2[:, c, :], FA[:, c, :], start=(c == 0), stop=(c == HC - 1))
                    if c == HC - 1:
                        ins.then_inc(full(key), 1)

                for half in range(2):
                    pe.wait_ge(*at(part + "_ln", b, 2))
                    up(half, 0)
                    yield from idle(2)
                    for c in range(HC):
                        if c + 1 < HC:
                            up(half, c + 1)
                        down(half, c)
                        yield from idle(2)

            def val(b, has_post, has_pre):
                if has_pre:
                    part_begins(graph_of(b, 1), "gat")
                else:
                    part_begins(graph_of(b, -2), "post")
                pe.wait_ge(*at("pre_ln", b, 4))
                for i in range(NT // 2):
                    key = ("v", i)
                    if not first_use(key):
                        pe.wait_ge(*bank_idle(b, key))
                    for j in range(2):
                        t = 2 * i + j
                        ins = nc.tensor.matmul(bank(key)[:, 256 * j:256 * (j + 1)], X2[:, t * P:(t + 1) * P],
                                               WV[:, :, :].rearrange("p w f -> p (w f)"), start=True, stop=True)
                    ins.then_inc(full(key), 1)
                    yield
                yield

            def post(b, in_loop):
                if in_loop:
                    part_begins(graph_of(b, 1), "val")
                else:
                    part_begins(graph_of(b, -1), "post")
                pe.wait_ge(*at("u_done", b, 2))
                key = ("sm",)
                for a in range(16):
                    ins = nc.tensor.matmul(bank(key)[:, 4 * a:4 * a + 4], U[:, a // 4, a % 4 * P:(a % 4 + 1) * P], SEL[:, :],
                                           start=True, stop=True)
                ins.then_inc(full(key), 1)
                yield from idle(3)
                for gi in range(4):
                    key = ("rb", gi)
                    pe.wait_ge(*at("rx_ready", b, gi + 1))
                    if not first_use(key):
                        pe.wait_ge(*bank_idle(b, key))
                    for c in range(4):
                        ins = nc.tensor.transpose(bank(key)[:, c * P:(c + 1) * P], AREAS["post"][0][:, gi, c * P:(c + 1) * P], IDF[:, :])
                    ins.then_inc(full(key), 1)
                    yield
                yield
                for gi in range(4):
                    pe.wait_ge(*bank_read(b, ("rb", gi)))
                for half in range(2):
                    key = ("wo", half)
                    pe.wait_ge(*bank_idle(b, key))
                    for g in range(2):
                        ins = nc.tensor.matmul(bank(key)[:, :], WO[:, g, :], U[:, 2 * g + half, :], start=(g == 0), stop=(g == 1))
                    ins.then_inc(full(key), 1)
                    yield
                yield
                yield from ln(b, 2, "post", lambda half: ("wo", half))
                yield from ff(b, 1, "post", W1, W2)
                yield from ln(b, 3, "post", lambda half: ("f2", 1, half))

            def gat(b):
                if is_graph(b, 2):
                    part_begins((0, 0), "val")
                elif not is_graph(b, 0) and not is_graph(b, 1):
                    part_begins(graph_of(b, -3), "post")
                for k in range(2):
                    h = (XT, H1)[k]
                    if k == 0:
                        pe.wait_ge(*at("x_in", b, 16))
                    else:
                        for half in range(2):
                            pe.wait_ge(*bank_read(b, ("gout", 0, half)))
                    for half in range(2):
                        key = ("s", k, half)
                        if not first_use(key):
                            pe.wait_ge(*bank_idle(b, key))
                        nc.tensor.matmul(bank(key)[:, :], WREP[:, k, :], h[:, hs(half)], start=True, stop=True).then_inc(full(key), 1)
                    yield
                    yield
                    for w in range(3):
                        key = ("wh", k, w)
                        if not first_use(key):
                            pe.wait_ge(*bank_idle(b, key))
                        for j in range(min(3, NT - 3 * w)):
                            t = 3 * w + j
                            ins = nc.tensor.matmul(bank(key)[:, j * (P + 1):(j + 1) * (P + 1)], h[:, t * P:(t + 1) * P],
                                                   WX[:, k, :], start=True, stop=True)
                        ins.then_inc(full(key), 1)
                        yield
                    yield from idle(3)
                    for t in range(NT):
                        pe.wait_ge(*at("whs_ready", b, NT * k + t + 1))
                        for half in range(2):
                            key = ("gout", k, half)
                            if t == 0:
                                pe.wait_ge(*bank_idle(b, key))
                            ins = nc.tensor.matmul(bank(key)[:, :], WHS[:, t % 4, :], LP[t % 5][:, half, :],
                                                   start=(t == 0), stop=(t == NT - 1))
                            if t == NT - 1:
                                ins.then_inc(full(key), 1)
                        if t < NT - 1:
                            ins.then_inc(sems["e_used"], 1)
                        yield
                    yield

            def pre(b, has_post):
                if not is_graph(b, 0) and not is_graph(b, 1):
                    pe.wait_ge(*at("u_done", graph_of(b, -1), 0))
                yield from ln(b, 0, "pre", lambda half: ("gout", 1, half), H1)
                yield from ff(b, 0, "pre", wff1, wff2)
                yield from ln(b, 1, "pre", lambda half: ("f2", 0, half))
                pe.wait_ge(*at("pre_ln", b, 4))
                for w, half in ((0, 0), (0, 1), (1, 0), (1, 1)):
                    key = ("qk"[w], half)
                    pe.wait_ge(*bank_idle(b, key))
                    nc.tensor.matmul(bank(key)[:, :], (Wq, Wk)[w], X2[:, hs(half)], start=True, stop=True).then_inc(full(key), 1)
                    if half == 1:
                        yield from idle(2)
                yield from idle(SPLIT)

            def whole_scores(b, tick, has_post):
                h, t = tick // NT, tick % NT
                if tick % (4 * NT) == 0:
                    pe.wait_ge(*at(f"stack_in{h // 4}", b, 16 * 2 * len(QK_PIECES)))
                if tick >= 2:
                    pe.wait_ge(*at("mx_read", b, tick - 1))
                elif has_post:
                    pe.wait_ge(*at("p_ready", b, 0))
                for half in range(2):
                    ins = nc.tensor.matmul(st[tick % 2][:, half, :], QS[0:KROWS, h, t * P:(t + 1) * P],
                                           KS[0:KROWS, h, hs(half)], start=True, stop=True)
                ins.then_inc(sems["mx_full"], 1)

            def transposed_maxima(b, g, has_post, has_pre):
                pe.wait_ge(*at("cm_ready", b, g + 1))
                if g == 1:
                    if has_pre:
                        part_begins(graph_of(b, 1), "pre")
                    elif has_post:
                        pe.wait_ge(*at("u_done", b, 0))
                ct = (st[(CT_TICK + 1) % 2][:, 0, :], pv[:, :])[g].bitcast(BF16)
                for t in range(NT):
                    ins = nc.tensor.transpose(ct[0:CROWS * 4, t * P:(t + 1) * P],
                                              CM[:, g, t, :, :].rearrange("p c h -> p (c h)"), IDB[:, :])
                ins.then_inc(sems["ct_full"], 1)

            def scores(b, n):
                g, it, t = n // (NHALF * NT), n // NT % NHALF, n % NT
                if n % (2 * NT) == 0:
                    pe.wait_ge(*at("c_in", b, 16 * CROWS * (g + 1)))
                for pr in range(2):
                    if n >= 1:
                        pe.wait_ge(*at("p_ready", b, 2 * (n - 1) + pr + 1))
                    else:
                        pe.wait_ge(*at("mx_read", b, MAX_TICKS - 1 + pr))
                    for x in range(2):
                        h = 4 * g + 2 * pr + x
                        ins = nc.tensor.matmul(st[pr][:, x, :], KS[0:SROWS, h, t * P:(t + 1) * P],
                                               QS[0:SROWS, h, hs(it)], start=True, stop=True)
                    ins.then_inc(sems["st_full"], 1)

            def products(n, w, exps):
                g, t = n // (NHALF * NT), n % NT
                for x in range(4):
                    ins = nc.tensor.matmul(pv[32 * x:32 * x + 32, :], v_of(t, w, 4 * g + x), exps[:, x, :],
                                           start=(t == 0 and w == 0), stop=(t == NT - 1 and w == 1))
                return ins

            def gather(b, n):
                gi, t = n // NT, n % NT
                if n == 0:
                    pe.wait_ge(*at("ct_read", b, 2))
                elif n == 2 * NT:
                    pe.wait_ge(*at("u_done", b, 1))
                elif t == 0:
                    pe.wait_ge(*at("u_ready", b, gi))
                pe.wait_ge(*at("p_ready", b, 2 * n + 2))
                products(n, 0, PT[:, n % 3])
                pe.wait_ge(*at("pm_ready", b, 2 * n + 2))
                products(n, 1, PM[:, n % 2]).then_inc(sems["p_used"], 1)

            def general_step(g, t, it, step):
                pe.wait_ge(*at_step("r_xb", step, 1))
                nc.tensor.matmul(pv[:, 0:3 * P], XB, WVX[:, :, :].rearrange("p r f -> p (r f)"),
                                 start=True, stop=True).then_inc(sems["r_v"], 1)
                for x in range(4):
                    ins = nc.tensor.matmul(
                        st[x // 2][:, x % 2, :],
                        KS[:, :, :].rearrange("p h (t n) -> p h t n", t=NT)[0:SROWS, 4 * g + x, t, :],
                        QS[:, :, :].rearrange("p h (i n) -> p h i n", i=NHALF)[0:SROWS, 4 * g + x, it, :],
                        start=True, stop=True)
                ins.then_inc(sems["r_st"], 1)
                pe.wait_ge(*at_step("r_vc", step, 1))
                for r in range(3):
                    pe.wait_ge(*at_step("r_pm", step, r + 1))
                    for x in range(4):
                        ins = nc.tensor.matmul(pv[32 * x:32 * x + 32, :], VC[:, r, x, :], PM[:, r % 2, x, :],
                                               start=(r == 0), stop=(r == 2))
                    ins.then_inc(sems["r_acc"], 1)

            def main(b, has_post, has_pre, has_gat):
                side = layers_of((gat, pre, val, post), b, has_post, has_pre)
                whole_scores(b, 0, has_post)
                for tick in range(MAX_TICKS):
                    if tick == CT_TICK:
                        pe.wait_ge(*at("mx_read", b, tick))
                        transposed_maxima(b, 0, has_post, has_pre)
                        pe.wait_ge(*at("ct_read", b, 1))
                    if tick == FLAG_TICK:
                        pe.wait_ge(*at("mx_read", b, tick))
                        pe.wait_ge(*at("am_seen", b, NT))
                        nc.tensor.matmul(st[(tick + 1) % 2][:, 0, 0:NT], MEAN[:, :], CHK[:, :],
                                         start=True, stop=True).then_inc(sems["fl_full"], 1)
                        pe.wait_ge(*at("fl_read", b, 1))
                    if tick + 1 < MAX_TICKS:
                        whole_scores(b, tick + 1, has_post)
                    next(side, None)
                rest(side)
                side = gat_of((gat, pre, val, post), b, has_gat)
                for n in range(ATT):
                    if n % (2 * NT) == 0:
                        scores(b, n)
                        if n == 0:
                            transposed_maxima(b, 1, has_post, has_pre)
                    if n % (2 * NT) != 0:
                        gather(b, n - 1)
                    if (n + 1) % (2 * NT) != 0:
                        scores(b, n + 1)
                    first_step(side, n)
                    if (n + 1) % (2 * NT) == 0:
                        gather(b, n)
                        g = n // (2 * NT)
                        pe.wait_ge(*at("u_ready", b, 2 * g + 2))
                        pe.wait_ge(*at("flag_ready", b, 1))
                        pe.sem_inc(flag_seen, 1)
                        flag = pe.value_load(FLAG[0:1, 0:1], min_val=0, max_val=1)
                        with pe.If(flag == 1):
                            with pe.Fori(0, NT) as tt:
                                with pe.Fori(0, NHALF) as ii:
                                    general_step(g, tt, ii, step_number(b, g, tt, ii))
                        with pe.Else():
                            for name in ("r_v", "r_st", "r_acc"):
                                pe.sem_inc(sems[name], per[name] // 2)
                    second_step(side, n)
                rest(side)

            rest(gat((0, 0)))
            rest(both(pre((0, 0), False), gat((0, 1))))
            main((0, 0), False, True, True)
            with pe.Fori(0, B - 3) as c:
                main((c, 1), True, True, True)
            main((0, B - 2), True, True, False)
            main((0, B - 1), True, False, False)
            rest(post((0, B - 1), False))


def kernel(**inputs):
    import numpy as np
    import concourse.bacc as bacc
    from concourse.bass_utils import run_bass_kernel_spmd as run

    a = {k: np.asarray(v) for k, v in inputs.items()}

    def chunks(w):
        return w.reshape(HC, P, F).transpose(1, 0, 2).reshape(P, HC * F)

    def by_dim(w):
        return w.reshape(-1, 2, NH // 2, DH).transpose(0, 1, 3, 2).reshape(-1, F)

    def column(v):
        return v.reshape(-1, P).T

    g1, g2 = a["L0_gnn_W1"], a["L0_gnn_W2"]
    a1, a2 = a["L0_gnn_a1"].reshape(2, F), a["L0_gnn_a2"].reshape(2, F)
    arrays = {
        "xT": a["x"].transpose(0, 2, 1),
        "adjT": a["adj"].transpose(0, 2, 1),
        "gwt": np.concatenate([g1.T, g2.T]),
        "mats": np.concatenate([g1, g2, a["L0_gnn_w_ff1"], chunks(a["L0_gnn_w_ff2"]),
                                by_dim(a["L1_gnn_Wq"]), by_dim(a["L1_gnn_Wk"]),
                                a["L1_gnn_W1"], chunks(a["L1_gnn_W2"])], axis=1),
        "wv": a["L1_gnn_Wv"].transpose(1, 0, 2),
        "wo": a["L1_gnn_Wo"],
        "cols": np.concatenate([column(v) for v in (
            a["L0_gnn_b_ff1"], a["L0_gnn_b_ff2"], a["L0_gnn_g_ln1"], a["L0_gnn_b_ln1"], a["L0_gnn_g_ln2"],
            a["L0_gnn_b_ln2"], by_dim(a["L1_gnn_bq"]), by_dim(a["L1_gnn_bk"]), a["L1_gnn_bo"], a["L1_gnn_b1"],
            a["L1_gnn_b2"], a["L1_gnn_g1"], a["L1_gnn_beta1"], a["L1_gnn_g2"], a["L1_gnn_beta2"],
            a1[0], a1[1], a2[0], a2[1])], axis=1),
        "bv": a["L1_gnn_bv"],
    }
    nc = bacc.Bacc("TRN2", target_bir_lowering=False, num_devices=1)
    given, args = {}, []
    for name, v in arrays.items():
        v = np.ascontiguousarray(v)
        given["in_" + name] = v
        args.append(nc.dram_tensor("in_" + name, v.shape, mybir.dt.from_np(v.dtype), kind="ExternalInput").ap())
    args.append(nc.dram_tensor("out_T", (B, F, N), F32, kind="ExternalOutput").ap())
    build(nc, *args)
    r = run(nc, [given], core_ids=[0])
    return np.ascontiguousarray(r.results[0]["out_T"].transpose(0, 2, 1))
```
